# Optimizing a Trainium2 kernel written in Bass

```python
import numpy as np
import jax
import jax.numpy as jnp

def _softmax(x, axis=-1):
    return jax.nn.softmax(x, axis=axis)

def _gelu(x):
    return jax.nn.gelu(x, approximate=True)

def _silu(x):
    return jax.nn.silu(x)

def _sigmoid(x):
    return jax.nn.sigmoid(x)

def _layernorm(x, axis=-1, eps=1e-05):
    m = jnp.mean(x, axis=axis, keepdims=True)
    v = jnp.var(x, axis=axis, keepdims=True)
    return (x - m) / jnp.sqrt(v + eps)

def _scatter_add(tgt, idx, src, axis=0):
    return tgt.at[idx].add(src)

def _segment_sum(src, seg, n):
    return jax.ops.segment_sum(src, seg, n)
kernel_name = 'mk_seq_preln_d1_jaxref_r8_b8c379'

def setup_inputs(seed: int=0):
    np.random.seed(seed)
    _w = jnp.asarray

    def _L0_attn_setup():
        import jax, jax.numpy as jnp
        import numpy as np
        EMBED_DIM = 128
        VALUE_DIM = 256
        NUM_HEADS = 8
        KEY_DIM = EMBED_DIM // NUM_HEADS
        HEAD_DIM = VALUE_DIM // NUM_HEADS
        EPS = 1e-05
        B, S = (2, 256)

        def _xavier(k, shape, gain):
            a = gain * np.sqrt(6.0 / (shape[0] + shape[1]))
            return jax.random.uniform(k, shape, jnp.float32, -a, a)

        def _rel_pos(slen):
            lin = jnp.linspace(0.0, 1.0, KEY_DIM // 2)
            angle = jnp.repeat(1.0 / 10000.0 ** lin, 2)
            decay = jnp.log1p(-2.0 ** (-5.0 - jnp.arange(NUM_HEADS, dtype=jnp.float32)))
            idx = jnp.arange(slen, dtype=jnp.float32)
            sin = jnp.sin(idx[:, None] * angle[None, :])
            cos = jnp.cos(idx[:, None] * angle[None, :])
            diff = idx[:, None] - idx[None, :]
            m = jnp.where(diff[None] >= 0, jnp.exp(diff[None] * decay[:, None, None]), 0.0)
            m = m / jnp.sqrt(m.sum(-1, keepdims=True))
            return (sin, cos, m)

        def _rotate_every_two(x):
            x1 = x[..., ::2]
            x2 = x[..., 1::2]
            return jnp.stack((-x2, x1), axis=-1).reshape(x.shape)
        key = jax.random.key(seed)
        ks = jax.random.split(key, 6)
        g = 2.0 ** (-2.5)
        return {'x': jax.random.normal(ks[0], (B, S, EMBED_DIM), jnp.float32), 'wq': _xavier(ks[1], (EMBED_DIM, EMBED_DIM), g), 'wk': _xavier(ks[2], (EMBED_DIM, EMBED_DIM), g), 'wv': _xavier(ks[3], (EMBED_DIM, VALUE_DIM), g), 'wg': _xavier(ks[4], (EMBED_DIM, VALUE_DIM), g), 'wo': _xavier(ks[5], (VALUE_DIM, EMBED_DIM), 1.0)}
    _L0_attn_in = _L0_attn_setup()

    def _L0_ffn_setup():
        import jax, jax.numpy as jnp
        import numpy as np
        NH, NKV, E, K = (16, 4, 8, 2)
        CAP_FACTOR = 1.25
        LN_EPS = 1e-05

        def _layer_norm(x, w, b):
            mu = jnp.mean(x, axis=-1, keepdims=True)
            var = jnp.mean(jnp.square(x - mu), axis=-1, keepdims=True)
            return (x - mu) * jax.lax.rsqrt(var + LN_EPS) * w + b
        key = jax.random.key(seed)
        ks = jax.random.split(key, 6)
        S, B, H, F = (256, 1, 128, 256)
        HD = H // NH
        qkv_out = NKV * (NH // NKV + 2) * HD
        f32 = jnp.float32
        return {'hidden_states': jax.random.normal(ks[0], (S, B, H), f32), 'ln1_weight': jnp.ones((H,), f32), 'ln1_bias': jnp.zeros((H,), f32), 'ln2_weight': jnp.ones((H,), f32), 'ln2_bias': jnp.zeros((H,), f32), 'qkv_weight': jax.random.normal(ks[1], (qkv_out, H), f32) * 0.02, 'proj_weight': jax.random.normal(ks[2], (H, H), f32) * 0.02, 'router_weight': jax.random.normal(ks[3], (H, E), f32) * 0.02, 'moe_w1': jax.random.normal(ks[4], (E, H, F), f32) * 0.02, 'moe_w2': jax.random.normal(ks[5], (F and E, F, H), f32)[:E] * 0.02 if False else jax.random.normal(ks[5], (E, F, H), f32) * 0.02}
    _L0_ffn_in = _L0_ffn_setup()
    _d = {'L0_attn_x': _L0_attn_in['x'], 'L0_attn_wq': _L0_attn_in['wq'], 'L0_attn_wk': _L0_attn_in['wk'], 'L0_attn_wv': _L0_attn_in['wv'], 'L0_attn_wg': _L0_attn_in['wg'], 'L0_attn_wo': _L0_attn_in['wo'], 'L0_ffn_ln1_weight': _L0_ffn_in['ln1_weight'], 'L0_ffn_ln1_bias': _L0_ffn_in['ln1_bias'], 'L0_ffn_ln2_weight': _L0_ffn_in['ln2_weight'], 'L0_ffn_ln2_bias': _L0_ffn_in['ln2_bias'], 'L0_ffn_qkv_weight': _L0_ffn_in['qkv_weight'], 'L0_ffn_proj_weight': _L0_ffn_in['proj_weight'], 'L0_ffn_router_weight': _L0_ffn_in['router_weight'], 'L0_ffn_moe_w1': _L0_ffn_in['moe_w1'], 'L0_ffn_moe_w2': _L0_ffn_in['moe_w2']}
    _x0 = _d['L0_attn_x']
    _d['L0_attn_x'] = jax.random.normal(jax.random.fold_in(jax.random.key(seed), 1), (8, 256, 128), dtype=_x0.dtype)
    del _x0
    return _d

def reference(L0_attn_x, L0_attn_wq, L0_attn_wk, L0_attn_wv, L0_attn_wg, L0_attn_wo, L0_ffn_ln1_weight, L0_ffn_ln1_bias, L0_ffn_ln2_weight, L0_ffn_ln2_bias, L0_ffn_qkv_weight, L0_ffn_proj_weight, L0_ffn_router_weight, L0_ffn_moe_w1, L0_ffn_moe_w2):

    def _L0_attn_ref(x, wq, wk, wv, wg, wo):
        import jax, jax.numpy as jnp
        import numpy as np
        EMBED_DIM = 128
        VALUE_DIM = 256
        NUM_HEADS = 8
        KEY_DIM = EMBED_DIM // NUM_HEADS
        HEAD_DIM = VALUE_DIM // NUM_HEADS
        EPS = 1e-05
        B, S = (2, 256)

        def _xavier(k, shape, gain):
            a = gain * np.sqrt(6.0 / (shape[0] + shape[1]))
            return jax.random.uniform(k, shape, jnp.float32, -a, a)

        def _rel_pos(slen):
            lin = jnp.linspace(0.0, 1.0, KEY_DIM // 2)
            angle = jnp.repeat(1.0 / 10000.0 ** lin, 2)
            decay = jnp.log1p(-2.0 ** (-5.0 - jnp.arange(NUM_HEADS, dtype=jnp.float32)))
            idx = jnp.arange(slen, dtype=jnp.float32)
            sin = jnp.sin(idx[:, None] * angle[None, :])
            cos = jnp.cos(idx[:, None] * angle[None, :])
            diff = idx[:, None] - idx[None, :]
            m = jnp.where(diff[None] >= 0, jnp.exp(diff[None] * decay[:, None, None]), 0.0)
            m = m / jnp.sqrt(m.sum(-1, keepdims=True))
            return (sin, cos, m)

        def _rotate_every_two(x):
            x1 = x[..., ::2]
            x2 = x[..., 1::2]
            return jnp.stack((-x2, x1), axis=-1).reshape(x.shape)
        b, s, _ = x.shape
        sin, cos, mask = _rel_pos(s)
        q = x @ wq
        k = x @ wk * KEY_DIM ** (-0.5)
        v = x @ wv
        g = x @ wg
        q = q.reshape(b, s, NUM_HEADS, KEY_DIM).transpose(0, 2, 1, 3)
        k = k.reshape(b, s, NUM_HEADS, KEY_DIM).transpose(0, 2, 1, 3)
        qr = q * cos + _rotate_every_two(q) * sin
        kr = k * cos + _rotate_every_two(k) * sin
        vr = v.reshape(b, s, NUM_HEADS, HEAD_DIM).transpose(0, 2, 1, 3)
        qk = jnp.einsum('bhik,bhjk->bhij', qr, kr) * mask[None]
        denom = jnp.clip(jnp.abs(jax.lax.stop_gradient(qk).sum(-1, keepdims=True)), 1.0, None)
        qk = qk / denom
        out = jnp.einsum('bhij,bhjd->bihd', qk, vr)
        out = out * jax.lax.rsqrt(jnp.mean(out * out, axis=-1, keepdims=True) + EPS)
        out = out.reshape(b, s, VALUE_DIM)
        out = jax.nn.silu(g) * out
        return out @ wo

    def _L0_ffn_ref(hidden_states, ln1_weight, ln1_bias, ln2_weight, ln2_bias, qkv_weight, proj_weight, router_weight, moe_w1, moe_w2):
        import jax, jax.numpy as jnp
        import numpy as np
        NH, NKV, E, K = (16, 4, 8, 2)
        CAP_FACTOR = 1.25
        LN_EPS = 1e-05

        def _layer_norm(x, w, b):
            mu = jnp.mean(x, axis=-1, keepdims=True)
            var = jnp.mean(jnp.square(x - mu), axis=-1, keepdims=True)
            return (x - mu) * jax.lax.rsqrt(var + LN_EPS) * w + b
        S, B, H = hidden_states.shape
        HD = H // NH
        q_per_kv = NH // NKV
        ln1 = _layer_norm(hidden_states, ln1_weight, ln1_bias)
        qkv = jnp.einsum('sbh,oh->sbo', ln1, qkv_weight)
        qkv = qkv.reshape(S, B, NKV, (q_per_kv + 2) * HD)
        q = qkv[..., :q_per_kv * HD].reshape(S, B, NH, HD)
        k = qkv[..., q_per_kv * HD:(q_per_kv + 1) * HD]
        v = qkv[..., (q_per_kv + 1) * HD:]
        qb = jnp.transpose(q, (1, 2, 0, 3)).reshape(B, NKV, q_per_kv, S, HD)
        kb = jnp.transpose(k, (1, 2, 0, 3))
        vb = jnp.transpose(v, (1, 2, 0, 3))
        scale = 1.0 / np.sqrt(HD).astype(np.float32)
        scores = jnp.einsum('bgqsd,bgtd->bgqst', qb, kb) * scale
        causal = jnp.tril(jnp.ones((S, S), bool))
        scores = jnp.where(causal, scores, jnp.finfo(scores.dtype).min)
        attn = jax.nn.softmax(scores, axis=-1)
        ao = jnp.einsum('bgqst,bgtd->bgqsd', attn, vb)
        ao = ao.reshape(B, NH, S, HD)
        ao = jnp.transpose(ao, (2, 0, 1, 3)).reshape(S, B, H)
        proj = jnp.einsum('sbh,oh->sbo', ao, proj_weight)
        h1 = hidden_states + proj
        ln2 = _layer_norm(h1, ln2_weight, ln2_bias)
        x = ln2.reshape(-1, H)
        N = x.shape[0]
        logits = x @ router_weight
        probs = jax.nn.softmax(logits, axis=-1)
        top_p, top_i = jax.lax.top_k(probs, K)
        top_p = top_p / jnp.sum(top_p, axis=-1, keepdims=True)
        exp_idx = top_i.reshape(-1)
        exp_p = top_p.reshape(-1)
        order = jnp.argsort(exp_idx, stable=True)
        sorted_exp = exp_idx[order]
        counts = jnp.bincount(exp_idx, length=E)
        offsets = jnp.concatenate([jnp.zeros((1,), counts.dtype), jnp.cumsum(counts)[:-1]])
        within = jnp.arange(N * K) - offsets[sorted_exp]
        cap = int(np.ceil(N * K / E * CAP_FACTOR))
        T = E * cap
        valid = within < cap
        dst = jnp.where(valid, sorted_exp * cap + within, T)
        padded_tokens = jnp.zeros((T, H), x.dtype).at[dst].set(x[order // K], mode='drop')
        padded_probs = jnp.zeros((T,), exp_p.dtype).at[dst].set(exp_p[order], mode='drop')
        padded_tid = jnp.zeros((T,), jnp.int32).at[dst].set((order // K).astype(jnp.int32), mode='drop')
        xt = padded_tokens.reshape(E, cap, H)
        fc1 = jax.nn.gelu(jnp.einsum('ech,ehf->ecf', xt, moe_w1))
        fc2 = jnp.einsum('ecf,efh->ech', fc1, moe_w2).reshape(T, H)
        weighted = fc2 * padded_probs[:, None]
        moe_out = jnp.zeros((N, H), hidden_states.dtype).at[padded_tid].add(weighted)
        return h1 + moe_out.reshape(S, B, H)
    x = L0_attn_x
    x = x + _L0_attn_ref(_layernorm(x, axis=-1), L0_attn_wq, L0_attn_wk, L0_attn_wv, L0_attn_wg, L0_attn_wo)
    x = x + _L0_ffn_ref(_layernorm(x, axis=-1), L0_ffn_ln1_weight, L0_ffn_ln1_bias, L0_ffn_ln2_weight, L0_ffn_ln2_bias, L0_ffn_qkv_weight, L0_ffn_proj_weight, L0_ffn_router_weight, L0_ffn_moe_w1, L0_ffn_moe_w2)
    return x

_drawn_inputs = setup_inputs


def setup_inputs(seed=0):
    import zlib

    import numpy as np

    out = dict(_drawn_inputs(seed))
    spreads = {'L0_ffn_ln1_weight': (1.0, 0.6),
     'L0_ffn_ln1_bias': (0.0, 0.8),
     'L0_ffn_ln2_weight': (1.0, 0.6),
     'L0_ffn_ln2_bias': (0.0, 0.8)}
    factors = {'L0_ffn_qkv_weight': 3.219,
     'L0_ffn_proj_weight': 3.088,
     'L0_ffn_router_weight': 4.701,
     'L0_ffn_moe_w1': 4.106,
     'L0_ffn_moe_w2': 4.011}
    for name, (base, spread) in spreads.items():
        noise = np.random.default_rng([zlib.crc32(name.encode()), seed]).standard_normal(out[name].shape)
        drawn = base * np.exp(spread * noise) if base else spread * noise
        out[name] = jnp.asarray(drawn.astype(out[name].dtype))
    for name, factor in factors.items():
        out[name] = (out[name] * factor).astype(out[name].dtype)
    return out
```

```python
from contextlib import ExitStack

import numpy as np

import concourse.bass as bass
from concourse import mybir

ALU = mybir.AluOpType
ACT = mybir.ActivationFunctionType
F32 = mybir.dt.float32
BF16 = mybir.dt.bfloat16
X = mybir.AxisListType.X

P = 128
NSEQ = 8
SLEN = 256
NC = SLEN // P
D = 128
VD = 256
RH = 8
RK = D // RH
RV = VD // RH
NH, NKV = 16, 4
QPK = NH // NKV
HD = D // NH
KVD = NKV * HD
NE = 8
F = 256
NF = F // P
TOPK = 2
CAP = -(-NSEQ * SLEN * TOPK * 5 // (NE * 4))
EPS = 1e-5
NEG = -3.0e38


ORDER = ("a_moments b_moments 0 a_T b_T 1 a_proj b_qkv 2 a_state 3 a_scores b_values 4 a_out b_proj 5 "
         "a_gated b_T2 6 a_wo b_router 7 b_gate 8").split()


def follow(stages, expert):
    for step in range(NSEQ + 2):
        for name in ORDER:
            i = step - (0 if name[0] == "a" else 1 if name[0] == "b" else 2)
            if not 0 <= i < NSEQ:
                continue
            if name.isdigit():
                expert(i, int(name))
            for stage in stages.get(name, ()):
                stage(i)


def retention_constants():
    lin = np.linspace(0.0, 1.0, RK // 2).astype(np.float32)
    angle = np.repeat((1.0 / np.float32(10000.0) ** lin).astype(np.float32), 2)
    decay = np.log1p(-2.0 ** (-5.0 - np.arange(RH)))
    idx = np.arange(SLEN)
    phase = (idx[:, None].astype(np.float32) * angle[None, :]).astype(np.float32).astype(np.float64)
    sin, cos = np.sin(phase), np.cos(phase)
    diff = idx[:, None] - idx[None, :]
    rows = np.stack([np.where(diff >= 0, np.exp(np.minimum(diff * -1.0, 0) * -decay[h]), 0).sum(-1)
                     for h in range(RH)])
    local = idx % P
    sign = np.where(np.arange(RK) % 2 == 0, -1.0, 1.0)
    fq = np.exp(local[None] * decay[:, None]) / np.sqrt(rows)
    fk = np.exp(-local[None] * decay[:, None]) * RK ** -0.5
    feat = lambda f, w: (f[:, None, :] * w.T[None]).reshape(D, SLEN)
    cos_t = np.concatenate([feat(fq, cos), feat(fk, cos)], 1)
    sin_t = np.concatenate([feat(fq, sin * sign), feat(fk, sin * sign)], 1)
    head_k, head_v = np.arange(D) // RK, np.arange(VD) // RV
    chunk_decay = np.exp(P * decay)[head_k][:, None]
    same = head_k[:, None] == head_v[None]
    parts = [cos_t, sin_t, same * chunk_decay, same * 1.0,
             (np.arange(P) // RV)[:, None] == (np.arange(P) // RV)[None],
             np.arange(P)[:, None] <= np.arange(P)[None],
             np.eye(P), head_k[:, None] == np.arange(RH)[None], chunk_decay, np.ones((P, P))]
    parts[4] = parts[4] * (1.0 / RV)
    return np.concatenate([np.asarray(p, np.float32) for p in parts], 1)


def routing_constants():
    lower = (np.arange(NE)[None] < np.arange(NE)[:, None]).reshape(1, NE * NE)
    return np.concatenate([np.arange(P)[:, None] < np.arange(P)[None], np.ones((P, P)),
                           np.repeat(lower, P, 0)], 1).astype(np.float32)


def build(nc, ins, out):
    ctx = ExitStack()
    with ctx:
        def sb(name, shape, dt=F32):
            return ctx.enter_context(nc.sbuf_tensor(name, shape, dt))

        class Signals:
            def __init__(self):
                self.made = {}

            def __call__(self, name):
                if name not in self.made:
                    self.made[name] = ctx.enter_context(nc.semaphore(name))
                return self.made[name]

        sem = Signals()

        wqk = sb("wqk", [P, 4, D])
        wv = sb("wv", [P, VD])
        wg = sb("wg", [P, VD])
        wo = sb("wo", [P, 2, D])
        wqkv = sb("wqkv", [P, D + 2 * KVD])
        wproj = sb("wproj", [P, D])
        wrouter = sb("wrouter", [P, NE])
        w1 = sb("w1", [P, NE, F])
        w2 = sb("w2", [P, NE, NF, D])
        lnp = sb("lnp", [P, 4])
        NCONST = ins["consts"].shape[1]
        con = sb("con", [P, NCONST])
        at = [0]

        def part(n):
            at[0] += n
            return con[:, at[0] - n:at[0]]

        cos_t, sin_t = part(2 * SLEN), part(2 * SLEN)
        state_mask, same_head, head_mean, tri, ident = part(VD), part(VD), part(P), part(P), part(P)
        head_sel, chunk_decay, ones = part(RH), part(1), part(P)
        rcon = sb("rcon", [P, 2 * P + NE * NE])
        before = sb("before", [P, 2 * P], BF16)
        lower = rcon[:, 2 * P:]

        x = sb("x", [P, NSEQ, NC, D])
        x1 = sb("x1", [P, NSEQ, NC, D])
        stat = sb("stat", [P, 2, NC, 6])
        mv = sb("mv", [P, 2, NC, 2])
        lnv = sb("lnv", [P, 2, NC])
        rstd = sb("rstd", [P, 2, NC])
        xh = sb("xh", [P, 2, NC, D])
        xT = sb("xT", [P, 2, SLEN])
        rot_a = sb("rot_a", [P, 2 * SLEN])
        rot_b = sb("rot_b", [P, 2 * SLEN])
        qk = sb("qk", [P, 2, 2, SLEN])
        qx = sb("qx", [P, NC, RH, P])
        v = sb("v", [P, 2, NC, VD])
        ag = sb("ag", [P, 2 * SLEN])
        ge = sb("ge", [P, 2 * SLEN])
        gl = sb("gl", [P, 2 * SLEN])
        gm = sb("gm", [P, 2 * SLEN])
        gT = sb("gT", [P, 2 * SLEN])
        kcum = sb("kcum", [P, SLEN])
        kinit = sb("kinit", [P, 1])
        qkc = sb("qkc", [P, SLEN])
        s2 = sb("s2", [P, 2 * SLEN])
        den = sb("den", [P, 2 * SLEN])
        knat = sb("knat", [P, P])
        state = sb("state", [P, VD])
        sm = sb("sm", [P, NC, RH, P])
        osq = sb("osq", [P, 2 * SLEN])
        tt = sb("tt", [P, 2 * SLEN])
        lt = sb("lt", [P, 2 * SLEN])
        z = sb("z", [P, 2 * SLEN])
        wgt = sb("wgt", [P, 2 * SLEN])
        og = sb("og", [P, 2 * SLEN])

        bstat = sb("bstat", [P, NC, 6])
        bmv = sb("bmv", [P, NC, 2])
        bv2 = sb("bv2", [P, NC, 2])
        bln = sb("bln", [P, NC, 2])
        br = sb("br", [P, NC, 2])
        hid = sb("hid", [P, NC, D])
        core = sb("core", [P, NC, D])
        l1T = sb("l1T", [P, SLEN])
        k4 = sb("k4", [P, NC, NSEQ, D])
        v4 = sb("v4", [P, NC, NSEQ, D])
        prod = sb("prod", [P, NC * NSEQ * D])
        prodv = sb("prodv", [P, NC * NSEQ * D])
        sc = sb("sc", [P, NC * NSEQ * NH])
        scm = sb("scm", [P, NC * NSEQ * NH])
        pe_ = sb("pe_", [P, NC * NSEQ * NH])
        mx = sb("mx", [P, NC, NH])
        ssum = sb("ssum", [P, NC, NH])
        rsum = sb("rsum", [P, NC, NH])
        ao = sb("ao", [P, NC, D])
        aon = sb("aon", [P, NC, D])
        aoT = sb("aoT", [P, SLEN])
        h1 = sb("h1", [P, NC, D])
        cstat = sb("cstat", [P, NC, 6])
        cmv = sb("cmv", [P, NC, 2])
        cv = sb("cv", [P, NC])
        cln = sb("cln", [P, NC])
        cr = sb("cr", [P, NC])
        core2 = sb("core2", [P, NC, D])
        x2T = sb("x2T", [P, 2, SLEN])
        lmx = sb("lmx", [P, NC])
        lsub = sb("lsub", [P, NC, NE])
        pr = sb("pr", [P, NC, NE])
        cgt = sb("cgt", [P, NC, NE, NE])
        cge = sb("cge", [P, NC, NE, NE])
        cgl = sb("cgl", [P, NC, NE, NE])
        cor = sb("cor", [P, NC, NE, NE])
        place = sb("place", [P, NC, NE])
        sel = sb("sel", [P, NC, NE])
        selb = sb("selb", [P, NC, NE], BF16)
        cum = sb("cum", [P, 2 * NSEQ + 1, NE], BF16)
        chosen = sb("chosen", [P, NC, NE])
        csum = sb("csum", [P, NC])
        crec = sb("crec", [P, NC])
        fits = sb("fits", [P, NC, NE])
        gsel = sb("gsel", [P, NC, NE])
        gate = sb("gate", [P, 2, NC, NE])
        base = sb("base", [P, 2, NC, D])
        hT = sb("hT", [P, 2, NF, SLEN])
        acc = sb("acc", [P, 2, 2, NC, D])
        res = sb("res", [P, 2, NC, D])

        ps = [ctx.enter_context(nc.psum_tensor(f"bank{i}", [P, 512], F32)) for i in range(8)]
        qk_ps, qks_ps, v_ps, g_ps = ps[0], ps[1], ps[2], ps[3]
        fc1_ps = [ps[4], ps[5]]
        fc2_ps = ps[6]
        b_ps = ps[7]

        x_dram = ins["x"].rearrange("s (c p) d -> p s c d", p=P)
        out_dram = out.rearrange("s (c p) d -> p s c d", p=P)
        block = ctx.enter_context(nc.Block())

        @block.sync
        def _(eng):
            def load(name, dst, src):
                eng.dma_start(dst, src).then_inc(sem(name), 16)

            load("x0_in", x[:, 0], x_dram[:, 0])
            load("con_in", con[:], ins["consts"])
            load("wqk_in", wqk[:], ins["wqk"].rearrange("f p n -> p f n"))
            load("wvg_in", wv[:], ins["wv"])
            load("wvg_in", wg[:], ins["wg"])
            load("wo_in", wo[:], ins["wo"].rearrange("(t p) n -> p t n", p=P))
            for i in range(1, NSEQ):
                load(f"x{i}_in", x[:, i], x_dram[:, i])
                if i == 1:
                    load("wb_in", wqkv[:], ins["wqkv"])
                    load("wb_in", wproj[:], ins["wproj"])
                    load("wb_in", wrouter[:], ins["wrouter"])
                    load("wb_in", lnp[:], ins["lnp"])
                    load("rcon_in", rcon[:], ins["rconsts"])
                    load("w1_in", w1[:], ins["w1"].rearrange("e p n -> p e n"))
                    load("w2_in", w2[:], ins["w2"].rearrange("e (t p) n -> p e t n", p=P))
            for i in range(NSEQ):
                eng.wait_ge(sem("acc"), NC * NE * (i + 1))
                eng.dma_start(out_dram[:, i], res[:, i % 2]).then_inc(sem(f"stored{i % 2}"), 16)
            eng.wait_ge(sem("stored0"), 16 * NSEQ // 2)
            eng.wait_ge(sem("stored1"), 16 * NSEQ // 2)

        @block.gpsimd
        def _(eng):
            eng.memset(cum[:, 0, :], 0.0).then_inc(sem("cum0"), 1)
            eng.wait_ge(sem("con_in"), 16)
            for i in range(NSEQ):
                eng.wait_ge(sem("rotated"), i + 1)
                if i >= 1:
                    eng.wait_ge(sem("scores"), 4 * i)
                for c in (1, 0):
                    for g in range(2):
                        hs = slice(4 * g, 4 * g + 4)
                        eng.tensor_tensor(
                            qx[:, c, hs, :],
                            qk[:, i % 2, 0, c * P:(c + 1) * P].unsqueeze(1).to_broadcast([P, 4, P]),
                            head_sel[:, hs].unsqueeze(2).to_broadcast([P, 4, P]),
                            ALU.mult).then_inc(sem("qx"), 1)

        @block.scalar
        def _(eng):
            def copy(o, i_, name):
                eng.copy(o, i_).then_inc(sem(name), 1)

            def norm_scale(o, tmp, var, ready, n, name):
                eng.wait_ge(sem(ready), n)
                eng.activation(tmp, var, ACT.Ln).then_inc(sem(name + "_ln"), 1)
                eng.wait_ge(sem(name + "_ln"), n)
                eng.activation(o, tmp, ACT.Exp, scale=-0.5).then_inc(sem(name), 1)

            def a_norm(i):
                norm_scale(rstd[:, i % 2], lnv[:, i % 2], mv[:, i % 2, :, 1], "a_var", i + 1, "a_rstd")

            def a_xT(i):
                eng.wait_ge(sem("a_T"), i + 1)
                copy(xT[:, i % 2], g_ps[:, 0:SLEN], "xT")

            def a_gate(i):
                if i >= 1:
                    eng.wait_ge(sem("og_raw"), i)
                copy(gT[:], g_ps[:], "gT")
                eng.activation(ag[:], g_ps[:], ACT.Abs).then_inc(sem("g_abs"), 1)
                eng.wait_ge(sem("g_abs"), i + 1)
                eng.activation(ge[:], ag[:], ACT.Exp, scale=-1.0).then_inc(sem("g_exp"), 1)
                eng.wait_ge(sem("g_exp"), i + 1)
                if i >= 1:
                    eng.wait_ge(sem("g_log_sig"), i)
                eng.activation(gl[:], ge[:], ACT.Ln, bias=1.0).then_inc(sem("g_ln"), 1)

            def a_v(i):
                eng.wait_ge(sem("vg"), i + 1)
                if i >= 2:
                    eng.wait_ge(sem("x1"), i - 1)
                copy(v[:, i % 2], v_ps[:].rearrange("p (c n) -> p c n", c=NC), "v")

            def a_knat(i):
                eng.wait_ge(sem("kT"), i + 1)
                copy(knat[:], qks_ps[:, 0:P], "knat")

            def a_s2(i):
                eng.wait_ge(sem("rowsum"), i + 1)
                if i >= 1:
                    eng.wait_ge(sem("den"), i)
                eng.activation(s2[:], qk_ps[:], ACT.Square).then_inc(sem("s2"), 1)

            def a_osq(i):
                eng.wait_ge(sem("o"), i + 1)
                eng.activation(osq[:], qk_ps[:], ACT.Square).then_inc(sem("osq"), 1)

            def a_scale(i):
                eng.wait_ge(sem("tt"), i + 1)
                eng.activation(lt[:], tt[:], ACT.Ln).then_inc(sem("lt"), 1)
                eng.wait_ge(sem("z"), i + 1)
                eng.activation(wgt[:], z[:], ACT.Exp).then_inc(sem("wgt"), 1)

            def b_norm(i):
                norm_scale(br[:], bln[:], bv2[:], "b_var", i + 1, "b_rstd")

            def b_l1T(i):
                eng.wait_ge(sem("b_T"), i + 1)
                eng.wait_ge(sem("wb_in"), 64)
                eng.activation(l1T[:], b_ps[:, 0:SLEN], ACT.Identity, bias=lnp[:, 1:2],
                               scale=lnp[:, 0:1]).then_inc(sem("l1T"), 1)

            def b_kv(i):
                eng.wait_ge(sem("qkv"), i + 1)
                for c in range(NC):
                    for dst, off in ((k4, D), (v4, D + KVD)):
                        src = b_ps[:, c * 192 + off:c * 192 + off + KVD]
                        src = src.rearrange("p (g d) -> p g d", d=HD).unsqueeze(2)
                        copy(dst[:, c, i].rearrange("p (g r d) -> p g r d", g=NKV, r=QPK),
                             src.to_broadcast([P, NKV, QPK, HD]), "kv4")

            def b_exp(i):
                n = NC * (i + 1) * NH
                eng.wait_ge(sem("scm"), i + 1)
                if i >= 1:
                    eng.wait_ge(sem("prodv"), i)
                eng.activation(pe_[:, 0:n], scm[:, 0:n], ACT.Exp, scale=HD ** -0.5).then_inc(sem("b_exp"), 1)

            def b_aoT(i):
                eng.wait_ge(sem("aoT_ps"), i + 1)
                copy(aoT[:], b_ps[:, 0:SLEN], "aoT")

            def c_norm(i):
                norm_scale(cr[:], cln[:], cv[:], "c_var", i + 1, "c_rstd")

            def c_x2T(i):
                eng.wait_ge(sem("c_T"), i + 1)
                eng.wait_ge(sem("wb_in"), 64)
                if i >= 2:
                    eng.wait_ge(sem("fc1"), NE * (i - 1))
                eng.activation(x2T[:, i % 2], b_ps[:, 0:SLEN], ACT.Identity, bias=lnp[:, 3:4],
                               scale=lnp[:, 2:3]).then_inc(sem("x2T"), 1)

            def c_exp(i):
                eng.wait_ge(sem("lsub"), i + 1)
                eng.activation(pr[:], lsub[:], ACT.Exp).then_inc(sem("pr"), 1)

            def m_gelu(i, e):
                n = NE * i + e
                eng.wait_ge(sem("fc1"), n + 1)
                if n >= 2:
                    eng.wait_ge(sem("fc2"), n - 1)
                eng.activation(hT[:, n % 2], fc1_ps[n % 2][:].rearrange("p (t n) -> p t n", t=NF),
                               ACT.Gelu_apprx_tanh).then_inc(sem("gelu"), 1)

            follow({
                "a_moments": [a_norm], "a_T": [a_xT], "a_proj": [a_v, a_gate], "a_state": [a_knat, a_s2],
                "a_out": [a_osq], "a_gated": [a_scale],
                "b_moments": [b_norm], "b_T": [b_l1T], "b_qkv": [b_kv, b_exp], "b_proj": [b_aoT, c_norm],
                "b_T2": [c_x2T], "b_router": [c_exp],
            }, lambda i, e: e < NE and m_gelu(i, e))

        @block.tensor
        def _(eng):
            mm = eng.matmul

            def a_T(i):
                eng.wait_ge(sem("a_xh"), NC * (i + 1))
                if i == 0:
                    eng.wait_ge(sem("con_in"), 16)
                if i >= 1:
                    eng.wait_ge(sem("x1"), i)
                for c in range(NC):
                    last = eng.transpose(g_ps[:, c * P:(c + 1) * P], xh[:, i % 2, c], ident)
                last.then_inc(sem("a_T"), 1)

            def a_proj(i):
                eng.wait_ge(sem("xT"), i + 1)
                t = xT[:, i % 2]
                if i == 0:
                    eng.wait_ge(sem("wqk_in"), 16)
                for f in range(4):
                    last = mm(ps[f // 2][:, (f % 2) * SLEN:(f % 2 + 1) * SLEN], wqk[:, f], t,
                              start=True, stop=True)
                last.then_inc(sem("qk"), 1)
                if i == 0:
                    eng.wait_ge(sem("wvg_in"), 32)
                for c in range(NC):
                    mm(v_ps[:, c * VD:(c + 1) * VD], t[:, c * P:(c + 1) * P], wv[:], start=True, stop=True)
                for u in range(2):
                    last = mm(g_ps[:, u * SLEN:(u + 1) * SLEN], wg[:, u * P:(u + 1) * P], t,
                              start=True, stop=True)
                last.then_inc(sem("vg"), 1)

            def a_state(i):
                eng.wait_ge(sem("rotated"), i + 1)
                eng.transpose(qks_ps[:, 0:P], qk[:, i % 2, 1, 0:P], ident).then_inc(sem("kT"), 1)
                eng.wait_ge(sem("qkc"), i + 1)
                for u in range(2):
                    last = mm(qk_ps[:, u * SLEN:(u + 1) * SLEN], same_head[:, u * P:(u + 1) * P], qkc[:],
                              start=True, stop=True)
                last.then_inc(sem("rowsum"), 1)
                eng.wait_ge(sem("knat"), i + 1)
                eng.wait_ge(sem("v"), i + 1)
                mm(qks_ps[:, P:P + VD], knat[:], v[:, i % 2, 0], start=True, stop=True).then_inc(sem("state_ps"), 1)

            def a_scores(i):
                for n, (c, g) in enumerate([(1, 0), (1, 1), (0, 0), (0, 1)]):
                    if n == 0:
                        eng.wait_ge(sem("v"), i + 1)
                        eng.wait_ge(sem("g_abs"), i + 1)
                    if n == 2:
                        eng.wait_ge(sem("s2"), i + 1)
                        eng.wait_ge(sem("state"), i + 1)
                    eng.wait_ge(sem("qx"), 4 * i + n + 1)
                    mm(ps[2 * c + g][:], qk[:, i % 2, 1, c * P:(c + 1) * P],
                       qx[:, c, 4 * g:4 * g + 4, :], start=True, stop=True).then_inc(sem("scores"), 1)

            def a_out(i):
                eng.wait_ge(sem("sm"), 4 * (i + 1))
                for u in range(2):
                    mm(qk_ps[:, u * SLEN + P:(u + 1) * SLEN], state[:, u * P:(u + 1) * P],
                       qk[:, i % 2, 0, P:SLEN], start=(u == 0), stop=False, skip_group_check=True)
                for c in range(NC):
                    for h in range(RH):
                        u, r = h // 4, h % 4
                        last = mm(qk_ps[32 * r:32 * r + 32, u * SLEN + c * P:u * SLEN + (c + 1) * P],
                                  v[:, i % 2, c, h * RV:(h + 1) * RV], sm[:, c, h, :],
                                  start=False, stop=(c == NC - 1 and u == 1), skip_group_check=True)
                last.then_inc(sem("o"), 1)

            def a_ms(i):
                eng.wait_ge(sem("osq"), i + 1)
                mm(qks_ps[:], head_mean, osq[:], start=True, stop=True).then_inc(sem("ms"), 1)

            def a_wo(i):
                eng.wait_ge(sem("og"), i + 1)
                if i == 0:
                    eng.wait_ge(sem("wo_in"), 16)
                for c in range(NC):
                    for u in range(2):
                        last = mm(v_ps[:, c * D:(c + 1) * D], og[:, u * SLEN + c * P:u * SLEN + (c + 1) * P],
                                  wo[:, u], start=(u == 0), stop=(u == 1))
                last.then_inc(sem("wo"), 1)

            def b_T(i):
                eng.wait_ge(sem("b_core"), NC * (i + 1))
                if i >= 1:
                    eng.wait_ge(sem("gate"), i)
                for c in range(NC):
                    last = eng.transpose(b_ps[:, c * P:(c + 1) * P], core[:, c], ident)
                last.then_inc(sem("b_T"), 1)

            def b_qkv(i):
                eng.wait_ge(sem("l1T"), i + 1)
                for c in range(NC):
                    last = mm(b_ps[:, c * 192:(c + 1) * 192], l1T[:, c * P:(c + 1) * P], wqkv[:],
                              start=True, stop=True)
                last.then_inc(sem("qkv"), 1)

            def b_aoT(i):
                eng.wait_ge(sem("aon"), i + 1)
                for c in range(NC):
                    last = eng.transpose(b_ps[:, c * P:(c + 1) * P], aon[:, c], ident)
                last.then_inc(sem("aoT_ps"), 1)
                eng.wait_ge(sem("aoT"), i + 1)
                for c in range(NC):
                    last = mm(b_ps[:, SLEN + c * P:SLEN + (c + 1) * P], aoT[:, c * P:(c + 1) * P], wproj[:],
                              start=True, stop=True)
                last.then_inc(sem("proj"), 1)

            def c_T(i):
                eng.wait_ge(sem("core2"), NC * (i + 1))
                for c in range(NC):
                    last = eng.transpose(b_ps[:, c * P:(c + 1) * P], core2[:, c], ident)
                last.then_inc(sem("c_T"), 1)

            def c_router(i):
                eng.wait_ge(sem("x2T"), i + 1)
                for c in range(NC):
                    last = mm(b_ps[:, SLEN + c * NE:SLEN + (c + 1) * NE], x2T[:, i % 2, c * P:(c + 1) * P],
                              wrouter[:], start=True, stop=True)
                last.then_inc(sem("logits"), 1)

            def c_rank(i):
                eng.wait_ge(sem("cum"), NC * (i + 1))
                for c in range(NC):
                    o = b_ps[:, SLEN + (NC + c) * NE:SLEN + (NC + c + 1) * NE]
                    mm(o, before[:, 0:P], selb[:, c], start=True, stop=False)
                    last = mm(o, before[:, P:], cum[:, NC * i + c, :], start=False, stop=True)
                last.then_inc(sem("rank"), 1)

            def m_fc1(i, e):
                n = NE * i + e
                if n >= 2:
                    eng.wait_ge(sem("gelu"), n - 1)
                if n == 0:
                    eng.wait_ge(sem("w1_in"), 16)
                if e == 0:
                    eng.wait_ge(sem("x2T"), i + 1)
                for t in range(NF):
                    last = mm(fc1_ps[n % 2][:, t * SLEN:(t + 1) * SLEN], w1[:, e, t * P:(t + 1) * P],
                              x2T[:, i % 2], start=True, stop=True)
                last.then_inc(sem("fc1"), 1)

            def m_fc2(i, e):
                n = NE * i + e
                eng.wait_ge(sem("gelu"), n + 1)
                if n == 0:
                    eng.wait_ge(sem("w2_in"), 16)
                if n >= 1:
                    eng.wait_ge(sem("acc"), NC * n)
                for c in range(NC):
                    for t in range(NF):
                        last = mm(fc2_ps[:, (n % 2) * SLEN + c * D:(n % 2) * SLEN + (c + 1) * D],
                                  hT[:, n % 2, t, c * P:(c + 1) * P], w2[:, e, t],
                                  start=(t == 0), stop=(t == NF - 1))
                last.then_inc(sem("fc2"), 1)

            def experts(i, e):
                if e < NE:
                    m_fc1(i, e)
                if e >= 1:
                    m_fc2(i, e - 1)

            follow({
                "a_T": [a_T], "a_proj": [a_proj], "a_state": [a_state], "a_scores": [a_scores],
                "a_out": [a_out], "a_gated": [a_ms], "a_wo": [a_wo],
                "b_T": [b_T], "b_qkv": [b_qkv], "b_proj": [b_aoT], "b_T2": [c_T], "b_router": [c_router],
                "b_gate": [c_rank],
            }, experts)

        @block.vector
        def _(eng):
            count = {}

            def done(ins_, name):
                ins_.then_inc(sem(name), 1)
                count[name] = count.get(name, 0) + 1

            def after(*names):
                for name in names:
                    eng.wait_ge(sem(name), count[name])

            tt_, ts_ = eng.tensor_tensor, eng.tensor_scalar

            def moments(src, st, out_, name):
                for c in range(NC):
                    done(eng.bn_stats(st[:, c], src[:, c]), name + "_stat")
                after(name + "_stat")
                for c in range(NC):
                    done(eng.bn_aggr(out_[:, c], st[:, c]), name + "_aggr")
                after(name + "_aggr")

            def a_moments(i):
                eng.wait_ge(sem(f"x{i}_in"), 16)
                moments(x[:, i], stat[:, i % 2], mv[:, i % 2], "a")
                done(ts_(mv[:, i % 2, :, 1], mv[:, i % 2, :, 1], EPS, None, ALU.add), "a_var")

            def a_xh(i):
                eng.wait_ge(sem("a_rstd"), i + 1)
                for c in range(NC):
                    done(ts_(xh[:, i % 2, c], x[:, i, c], mv[:, i % 2, c, 0:1], rstd[:, i % 2, c:c + 1],
                             ALU.subtract, ALU.mult), "a_xh")

            def a_rotate(i):
                eng.wait_ge(sem("qk"), i + 1)
                done(tt_(rot_a[:], qk_ps[:], cos_t, ALU.mult), "rot_a")
                done(tt_(rot_b[:], qks_ps[:], sin_t, ALU.mult), "rot_b")
                after("rot_b")
                done(tt_(qk[:, i % 2].rearrange("p f n -> p (f n)"), rot_a[:], rot_b[:], ALU.add), "rotated")

            def a_rowsum(i):
                after("rotated")
                k = qk[:, i % 2, 1]
                done(eng.tensor_tensor_scan(kcum[:, 0:P], ones, k[:, 0:P], 0.0, ALU.mult, ALU.add), "kc0")
                after("kc0")
                done(tt_(kinit[:], kcum[:, P - 1:P], chunk_decay, ALU.mult), "kinit")
                after("kinit")
                done(eng.tensor_tensor_scan(kcum[:, P:SLEN], ones, k[:, P:SLEN], kinit[:], ALU.mult, ALU.add), "kc1")
                after("kc1")
                done(tt_(qkc[:], qk[:, i % 2, 0], kcum[:], ALU.mult), "qkc")

            def a_gate(i):
                eng.wait_ge(sem("g_ln"), i + 1)
                done(eng.scalar_tensor_tensor(gm[:], gT[:], 0.0, gl[:], ALU.min, ALU.subtract), "g_log_sig")

            def a_state(i):
                eng.wait_ge(sem("s2"), i + 1)
                done(ts_(den[:], s2[:], 1.0, EPS, ALU.max, ALU.mult), "den")
                eng.wait_ge(sem("state_ps"), i + 1)
                done(tt_(state[:], qks_ps[:, P:P + VD], state_mask, ALU.mult), "state")

            def a_mask(i):
                for n, (c, g) in enumerate([(1, 0), (1, 1), (0, 0), (0, 1)]):
                    eng.wait_ge(sem("scores"), 4 * i + n + 1)
                    done(tt_(sm[:, c, 4 * g:4 * g + 4, :], ps[2 * c + g][:].rearrange("p (h n) -> p h n", h=4),
                             tri.unsqueeze(1).to_broadcast([P, 4, P]), ALU.mult), "sm")

            def a_norm(i):
                eng.wait_ge(sem("ms"), i + 1)
                after("den")
                done(tt_(tt[:], qks_ps[:], den[:], ALU.add), "tt")
                eng.wait_ge(sem("lt"), i + 1)
                after("g_log_sig")
                done(eng.scalar_tensor_tensor(z[:], lt[:], -0.5, gm[:], ALU.mult, ALU.add), "z")
                done(tt_(og[:], qk_ps[:], gT[:], ALU.mult), "og_raw")
                eng.wait_ge(sem("wgt"), i + 1)
                after("og_raw")
                done(tt_(og[:], og[:], wgt[:], ALU.mult), "og")

            def a_x1(i):
                eng.wait_ge(sem("wo"), i + 1)
                done(tt_(x1[:, i], v_ps[:, 0:SLEN].rearrange("p (c n) -> p c n", c=NC), x[:, i], ALU.add), "x1")

            def b_moments(i):
                after("x1")
                moments(x1[:, i], bstat, bmv, "b")
                done(ts_(bv2[:, :, 0], bmv[:, :, 1], EPS, None, ALU.add), "b_var0")
                done(ts_(bv2[:, :, 1], bmv[:, :, 1], 1.0 + EPS, EPS * EPS, ALU.mult, ALU.add), "b_var")

            def b_core(i):
                eng.wait_ge(sem("b_rstd"), i + 1)
                for c in range(NC):
                    done(ts_(core[:, c], x1[:, i, c], bmv[:, c, 0:1], br[:, c, 1:2],
                             ALU.subtract, ALU.mult), "b_core")
                for c in range(NC):
                    done(ts_(hid[:, c], x1[:, i, c], bmv[:, c, 0:1], br[:, c, 0:1],
                             ALU.subtract, ALU.mult), "hid")

            def b_scores(i):
                n = i + 1
                eng.wait_ge(sem("kv4"), 4 * n)
                q = b_ps[:, 0:2 * 192].rearrange("p (c n) -> p c n", c=NC)[:, :, 0:D]
                pv = prod[:, 0:NC * n * D]
                done(tt_(pv.rearrange("p (c t f) -> p c t f", c=NC, t=n),
                         q.unsqueeze(2).to_broadcast([P, NC, n, D]), k4[:, :, 0:n, :], ALU.mult), "prod")
                after("prod")
                done(eng.tensor_reduce(sc[:, 0:NC * n * NH], pv.rearrange("p (a d) -> p a d", d=HD), X, ALU.add), "sc")
                after("sc")
                s = sc[:, 0:NC * n * NH].rearrange("p (c t h) -> p c t h", c=NC, t=n)
                done(eng.tensor_reduce(mx[:], s.rearrange("p c t h -> p c h t"), X, ALU.max), "mx")
                after("mx")
                done(tt_(scm[:, 0:NC * n * NH].rearrange("p (c t h) -> p c t h", c=NC, t=n), s,
                         mx[:].unsqueeze(2).to_broadcast([P, NC, n, NH]), ALU.subtract), "scm")

            def b_values(i):
                n = i + 1
                eng.wait_ge(sem("b_exp"), n)
                e = pe_[:, 0:NC * n * NH]
                pv = prodv[:, 0:NC * n * D]
                for c in range(NC):
                    ec = e[:, c * n * NH:(c + 1) * n * NH]
                    ins_ = tt_(pv[:, c * n * D:(c + 1) * n * D].rearrange("p (a d) -> p a d", d=HD),
                               ec.unsqueeze(2).to_broadcast([P, n * NH, HD]),
                               v4[:, c, 0:n, :].rearrange("p t (h d) -> p (t h) d", d=HD), ALU.mult)
                    if c == NC - 1:
                        done(ins_, "prodv")
                done(eng.tensor_reduce(ssum[:], e.rearrange("p (c t h) -> p c h t", c=NC, t=n), X, ALU.add), "ssum")
                after("ssum")
                done(eng.reciprocal(rsum[:], ssum[:]), "rsum")
                after("prodv")
                done(eng.tensor_reduce(ao[:], pv.rearrange("p (c t f) -> p c f t", c=NC, t=n), X, ALU.add), "ao")
                after("ao", "rsum")
                done(tt_(aon[:].rearrange("p c (h d) -> p (c h) d", d=HD),
                         ao[:].rearrange("p c (h d) -> p (c h) d", d=HD),
                         rsum[:].rearrange("p c h -> p (c h)").unsqueeze(2).to_broadcast([P, NC * NH, HD]),
                         ALU.mult), "aon")

            def c_h1(i):
                eng.wait_ge(sem("proj"), i + 1)
                after("hid")
                done(tt_(h1[:], b_ps[:, SLEN:2 * SLEN].rearrange("p (c n) -> p c n", c=NC), hid[:], ALU.add), "h1")
                after("h1")
                moments(h1, cstat, cmv, "c")
                done(ts_(cv[:], cmv[:, :, 1], EPS, None, ALU.add), "c_var")
                done(tt_(base[:, i % 2], h1[:], x1[:, i], ALU.add), "base")

            def c_core(i):
                eng.wait_ge(sem("c_rstd"), i + 1)
                for c in range(NC):
                    done(ts_(core2[:, c], h1[:, c], cmv[:, c, 0:1], cr[:, c:c + 1],
                             ALU.subtract, ALU.mult), "core2")

            def c_lsub(i):
                eng.wait_ge(sem("logits"), i + 1)
                lg = b_ps[:, SLEN:SLEN + NC * NE].rearrange("p (c e) -> p c e", c=NC)
                done(eng.tensor_reduce(lmx[:], lg, X, ALU.max), "lmx")
                after("lmx")
                done(tt_(lsub[:], lg, lmx[:].unsqueeze(2).to_broadcast([P, NC, NE]), ALU.subtract), "lsub")

            def c_select(i):
                if i == 0:
                    eng.wait_ge(sem("rcon_in"), 16)
                    done(eng.tensor_copy(before[:], rcon[:, 0:2 * P]), "before")
                    eng.wait_ge(sem("cum0"), 1)
                eng.wait_ge(sem("pr"), i + 1)
                low = lower.rearrange("p (e j) -> p e j", e=NE)
                for c in range(NC):
                    mine = pr[:, c].unsqueeze(2).to_broadcast([P, NE, NE])
                    other = pr[:, c].unsqueeze(1).to_broadcast([P, NE, NE])
                    done(tt_(cgt[:, c], other, mine, ALU.is_gt), "cgt")
                    done(tt_(cge[:, c], other, mine, ALU.is_ge), "cge")
                after("cge")
                done(tt_(cgl[:], cge[:], low.unsqueeze(1).to_broadcast([P, NC, NE, NE]), ALU.mult), "cgl")
                after("cgl")
                done(tt_(cor[:], cgl[:], cgt[:], ALU.max), "cor")
                after("cor")
                done(eng.tensor_reduce(place[:], cor[:], X, ALU.add), "place")
                after("place")
                done(ts_(selb[:], place[:], TOPK - 0.5, None, ALU.is_lt), "selb")
                done(ts_(sel[:], place[:], TOPK - 0.5, None, ALU.is_lt), "sel")
                after("sel")
                for c in range(NC):
                    n = NC * i + c
                    done(tt_(cum[:, n + 1, :], cum[:, n, :], selb[:, c], ALU.add), "cum")
                    after("cum")
                done(tt_(chosen[:], pr[:], sel[:], ALU.mult), "chosen")
                after("chosen")
                done(eng.tensor_reduce(csum[:], chosen[:], X, ALU.add), "csum")
                after("csum")
                done(eng.reciprocal(crec[:], csum[:]), "crec")
                after("crec")
                done(tt_(gsel[:], chosen[:], crec[:].unsqueeze(2).to_broadcast([P, NC, NE]), ALU.mult), "gsel")

            def c_gate(i):
                eng.wait_ge(sem("rank"), i + 1)
                rk = b_ps[:, SLEN + NC * NE:SLEN + 2 * NC * NE].rearrange("p (c e) -> p c e", c=NC)
                done(ts_(fits[:], rk, CAP - 0.5, None, ALU.is_lt), "fits")
                after("fits", "gsel")
                done(tt_(gate[:, i % 2], gsel[:], fits[:], ALU.mult), "gate")

            def m_acc(i, e):
                n = NE * i + e
                eng.wait_ge(sem("fc2"), n + 1)
                if e == 0:
                    after("gate", "base")
                else:
                    after("acc")
                if e == NE - 1 and i >= 2:
                    eng.wait_ge(sem(f"stored{i % 2}"), 16 * (i // 2))
                for c in range(NC):
                    o = fc2_ps[:, (n % 2) * SLEN + c * D:(n % 2) * SLEN + (c + 1) * D]
                    prev = base[:, i % 2, c] if e == 0 else acc[:, i % 2, (e - 1) % 2, c]
                    dst = res[:, i % 2, c] if e == NE - 1 else acc[:, i % 2, e % 2, c]
                    done(eng.scalar_tensor_tensor(dst, o, gate[:, i % 2, c, e:e + 1], prev,
                                                  ALU.mult, ALU.add), "acc")

            eng.wait_ge(sem("con_in"), 16)
            follow({
                "a_moments": [a_moments], "a_T": [a_xh], "a_proj": [a_rotate, a_rowsum, a_gate],
                "a_state": [a_state], "a_scores": [a_mask], "a_gated": [a_norm], "a_wo": [a_x1],
                "b_moments": [b_moments], "b_T": [b_core], "b_qkv": [b_scores], "b_values": [b_values],
                "b_proj": [c_h1], "b_T2": [c_core], "b_router": [c_lsub], "b_gate": [c_select, c_gate],
            }, lambda i, e: e >= 1 and m_acc(i, e - 1))


def lay_out(a):
    f = lambda n: np.ascontiguousarray(np.asarray(a[n]))
    wq, wk = f("L0_attn_wq"), f("L0_attn_wk")
    swap = np.arange(D) ^ 1
    per = f("L0_ffn_qkv_weight").reshape(NKV, (QPK + 2) * HD, D)
    q, k, v = per[:, :QPK * HD], per[:, QPK * HD:(QPK + 1) * HD], per[:, (QPK + 1) * HD:]
    return {
        "x": f("L0_attn_x"),
        "consts": retention_constants(),
        "rconsts": routing_constants(),
        "wqk": np.stack([wq, wk, wq[:, swap], wk[:, swap]]),
        "wv": f("L0_attn_wv"), "wg": f("L0_attn_wg"), "wo": f("L0_attn_wo"),
        "wqkv": np.concatenate([t.reshape(-1, D) for t in (q, k, v)]).T,
        "wproj": f("L0_ffn_proj_weight").T,
        "wrouter": f("L0_ffn_router_weight"),
        "lnp": np.stack([f("L0_ffn_ln1_weight"), f("L0_ffn_ln1_bias"), f("L0_ffn_ln2_weight"), f("L0_ffn_ln2_bias")], 1),
        "w1": f("L0_ffn_moe_w1"), "w2": f("L0_ffn_moe_w2"),
    }


def kernel(**inputs):
    import concourse.bacc as _bacc
    from concourse.bass_utils import run_bass_kernel_spmd as _run

    nc = _bacc.Bacc("TRN2", target_bir_lowering=False, num_devices=1)
    arrays = {f"in_{n}": np.ascontiguousarray(a) for n, a in lay_out(inputs).items()}
    ins = {n[3:]: nc.dram_tensor(n, a.shape, mybir.dt.from_np(a.dtype), kind="ExternalInput").ap()
           for n, a in arrays.items()}
    out = nc.dram_tensor("out", (NSEQ, SLEN, D), F32, kind="ExternalOutput").ap()
    build(nc, ins, out)
    r = _run(nc, [arrays], core_ids=[0])
    return r.results[0]["out"]
```

```python
from contextlib import ExitStack

import numpy as np

import concourse.bass as bass
from concourse import mybir

ALU = mybir.AluOpType
ACT = mybir.ActivationFunctionType
F32 = mybir.dt.float32
BF16 = mybir.dt.bfloat16
X = mybir.AxisListType.X

P = 128
NSEQ = 8
SLEN = 256
NC = SLEN // P
D = 128
VD = 256
RH = 8
RK = D // RH
RV = VD // RH
NH, NKV = 16, 4
QPK = NH // NKV
HD = D // NH
KVD = NKV * HD
NE = 8
F = 256
NF = F // P
TOPK = 2
CAP = -(-NSEQ * SLEN * TOPK * 5 // (NE * 4))
EPS = 1e-5
NEG = -3.0e38


ORDER = """
a_weight@1 a_og@1 c_rstd@1 m_gelu_5@1 c_core@1 m_acc_4@1 m_fc1_6@1 a_wo@1 m_gelu_6@1 c_T@1 c_x2T@1
m_fc2_5@1 a_moments c_logits@1 a_x1@1 b_moments c_lsub@1 c_exp@1 a_rstd m_acc_5@1 m_fc1_7@1
m_fc2_6@1 m_fc1_0 c_place@1 a_xh a_T m_acc_6@1 b_rstd m_gelu_7@1 c_select@1 a_xT m_fc2_7@1 c_rank@1
b_base@1 c_gsel@1 m_gelu_0 a_qk c_gate@1 b_core a_vg m_acc_7@1 a_gT b_T b_l1T a_v b_qkv b_kv4
a_rotate a_kcum m_fc1_1 b_scores a_kT a_qkc m_fc2_0 m_acc_0 b_scores2 a_knat a_rowsums m_gelu_1
a_sigmoid m_fc1_2 a_qx b_exp a_state_mm m_fc2_1 m_acc_1 a_state a_s2 a_log_sigmoid m_fc1_3 m_gelu_2
b_sum b_prodv m_gelu_3 a_scores a_mask m_fc2_2 a_out a_osq m_acc_2 m_fc1_4 b_ao b_norm a_ms a_den
a_scale_in m_gelu_4 a_ln a_og_raw m_fc2_3 m_acc_3 a_z b_aoT_mm b_aoT b_proj m_fc1_5 b_h1 c_moments
m_fc2_4
""".split()
LAG = {"a": 0, "b": 1, "c": 1, "m": 2}


def follow(stages):
    order = [(name, LAG[name[0]] + int(late or 0)) for name, _, late in (x.partition("@") for x in ORDER)]
    for step in range(NSEQ + 1 + max(lag for _, lag in order)):
        for name, lag in order:
            if name in stages and 0 <= step - lag < NSEQ:
                stages[name](step - lag)


def retention_constants():
    lin = np.linspace(0.0, 1.0, RK // 2).astype(np.float32)
    angle = np.repeat((1.0 / np.float32(10000.0) ** lin).astype(np.float32), 2)
    decay = np.log1p(-2.0 ** (-5.0 - np.arange(RH)))
    idx = np.arange(SLEN)
    phase = (idx[:, None].astype(np.float32) * angle[None, :]).astype(np.float32).astype(np.float64)
    sin, cos = np.sin(phase), np.cos(phase)
    diff = idx[:, None] - idx[None, :]
    rows = np.stack([np.where(diff >= 0, np.exp(np.minimum(diff * -1.0, 0) * -decay[h]), 0).sum(-1)
                     for h in range(RH)])
    local = idx % P
    sign = np.where(np.arange(RK) % 2 == 0, -1.0, 1.0)
    fq = np.exp(local[None] * decay[:, None]) / np.sqrt(rows)
    fk = np.exp(-local[None] * decay[:, None]) * RK ** -0.5
    feat = lambda f, w: (f[:, None, :] * w.T[None]).reshape(D, SLEN)
    cos_t = np.concatenate([feat(fq, cos), feat(fk, cos)], 1)
    sin_t = np.concatenate([feat(fq, sin * sign), feat(fk, sin * sign)], 1)
    head_k, head_v = np.arange(D) // RK, np.arange(VD) // RV
    chunk_decay = np.exp(P * decay)[head_k][:, None]
    same = head_k[:, None] == head_v[None]
    parts = [cos_t, sin_t, same * chunk_decay, same * 1.0,
             (np.arange(P) // RV)[:, None] == (np.arange(P) // RV)[None],
             np.arange(P)[:, None] <= np.arange(P)[None],
             np.eye(P), head_k[:, None] == np.arange(RH)[None], chunk_decay, np.ones((P, P))]
    parts[4] = parts[4] * (1.0 / RV)
    return np.concatenate([np.asarray(p, np.float32) for p in parts], 1)


def routing_constants():
    lower = (np.arange(NE)[None] < np.arange(NE)[:, None]).reshape(1, NE * NE)
    return np.concatenate([np.arange(P)[:, None] < np.arange(P)[None], np.ones((P, P)),
                           np.repeat(lower, P, 0)], 1).astype(np.float32)


def build(nc, ins, out):
    ctx = ExitStack()
    with ctx:
        def sb(name, shape, dt=F32):
            return ctx.enter_context(nc.sbuf_tensor(name, shape, dt))

        class Signals:
            def __init__(self):
                self.made = {}

            def __call__(self, name):
                if name not in self.made:
                    self.made[name] = ctx.enter_context(nc.semaphore(name))
                return self.made[name]

        sem = Signals()

        wqk = sb("wqk", [P, 4, D])
        wv = sb("wv", [P, VD])
        wg = sb("wg", [P, VD])
        wo = sb("wo", [P, 2, D])
        wqkv = sb("wqkv", [P, D + 2 * KVD])
        wproj = sb("wproj", [P, D])
        wrouter = sb("wrouter", [P, NE])
        w1 = sb("w1", [P, NE, F])
        w2 = sb("w2", [P, NE, NF, D])
        lnp = sb("lnp", [P, 4])
        NCONST = ins["consts"].shape[1]
        con = sb("con", [P, NCONST])
        at = [0]

        def part(n):
            at[0] += n
            return con[:, at[0] - n:at[0]]

        cos_t, sin_t = part(2 * SLEN), part(2 * SLEN)
        state_mask, same_head, head_mean, tri, ident = part(VD), part(VD), part(P), part(P), part(P)
        head_sel, chunk_decay, ones = part(RH), part(1), part(P)
        rcon = sb("rcon", [P, 2 * P + NE * NE])
        before = sb("before", [P, 2 * P], BF16)
        lower = rcon[:, 2 * P:]

        x = sb("x", [P, NSEQ, NC, D])
        x1 = sb("x1", [P, NSEQ, NC, D])
        stat = sb("stat", [P, 2, NC, 6])
        mv = sb("mv", [P, 2, NC, 2])
        lnv = sb("lnv", [P, 2, NC])
        rstd = sb("rstd", [P, 2, NC])
        xh = sb("xh", [P, 2, NC, D])
        xT = sb("xT", [P, 2, SLEN])
        rot_a = sb("rot_a", [P, 2 * SLEN])
        rot_b = sb("rot_b", [P, 2 * SLEN])
        qk = sb("qk", [P, 2, 2, SLEN])
        qx = sb("qx", [P, NC, RH, P])
        v = sb("v", [P, 2, NC, VD])
        ag = sb("ag", [P, 2 * SLEN])
        ge = sb("ge", [P, 2 * SLEN])
        gl = sb("gl", [P, 2 * SLEN])
        gm = sb("gm", [P, 2 * SLEN])
        gT = sb("gT", [P, 2 * SLEN])
        kcum = sb("kcum", [P, SLEN])
        kinit = sb("kinit", [P, 1])
        qkc = sb("qkc", [P, SLEN])
        s2 = sb("s2", [P, 2 * SLEN])
        den = sb("den", [P, 2 * SLEN])
        knat = sb("knat", [P, P])
        state = sb("state", [P, VD])
        sm = sb("sm", [P, NC, RH, P])
        osq = sb("osq", [P, 2 * SLEN])
        tt = sb("tt", [P, 2 * SLEN])
        lt = sb("lt", [P, 2 * SLEN])
        z = sb("z", [P, 2 * SLEN])
        wgt = sb("wgt", [P, 2 * SLEN])
        og = sb("og", [P, 2 * SLEN])

        bstat = sb("bstat", [P, NC, 6])
        bmv = sb("bmv", [P, NC, 2])
        bv2 = sb("bv2", [P, NC, 2])
        bln = sb("bln", [P, NC, 2])
        br = sb("br", [P, NC, 2])
        hid = sb("hid", [P, NC, D])
        core = sb("core", [P, NC, D])
        l1T = sb("l1T", [P, SLEN])
        k4 = sb("k4", [P, NC, NSEQ, D])
        v4 = sb("v4", [P, NC, NSEQ, D])
        prod = sb("prod", [P, NC * NSEQ * D])
        prodv = sb("prodv", [P, NC * NSEQ * D])
        sc = sb("sc", [P, NC * NSEQ * NH])
        scm = sb("scm", [P, NC * NSEQ * NH])
        pe_ = sb("pe_", [P, NC * NSEQ * NH])
        mx = sb("mx", [P, NC, NH])
        ssum = sb("ssum", [P, NC, NH])
        rsum = sb("rsum", [P, NC, NH])
        ao = sb("ao", [P, NC, D])
        aon = sb("aon", [P, NC, D])
        aoT = sb("aoT", [P, SLEN])
        h1 = sb("h1", [P, NC, D])
        cstat = sb("cstat", [P, NC, 6])
        cmv = sb("cmv", [P, NC, 2])
        cv = sb("cv", [P, NC])
        cln = sb("cln", [P, NC])
        cr = sb("cr", [P, NC])
        core2 = sb("core2", [P, NC, D])
        x2T = sb("x2T", [P, 2, SLEN])
        lmx = sb("lmx", [P, NC])
        lsub = sb("lsub", [P, NC, NE])
        pr = sb("pr", [P, NC, NE])
        cgt = sb("cgt", [P, NC, NE, NE])
        cge = sb("cge", [P, NC, NE, NE])
        cgl = sb("cgl", [P, NC, NE, NE])
        cor = sb("cor", [P, NC, NE, NE])
        place = sb("place", [P, NC, NE])
        sel = sb("sel", [P, NC, NE])
        selb = sb("selb", [P, NC, NE], BF16)
        cum = sb("cum", [P, 2 * NSEQ + 1, NE], BF16)
        chosen = sb("chosen", [P, NC, NE])
        csum = sb("csum", [P, NC])
        crec = sb("crec", [P, NC])
        fits = sb("fits", [P, NC, NE])
        gsel = sb("gsel", [P, NC, NE])
        gate = sb("gate", [P, 2, NC, NE])
        base = sb("base", [P, 2, NC, D])
        hT = sb("hT", [P, 2, NF, SLEN])
        acc = sb("acc", [P, 2, 2, NC, D])
        res = sb("res", [P, 2, NC, D])

        ps = [ctx.enter_context(nc.psum_tensor(f"bank{i}", [P, 512], F32)) for i in range(8)]
        qk_ps, qks_ps, v_ps, g_ps = ps[0], ps[1], ps[2], ps[3]
        fc1_ps = [ps[4], ps[5]]
        fc2_ps = ps[6]
        b_ps = ps[7]

        x_dram = ins["x"].rearrange("s (c p) d -> p s c d", p=P)
        out_dram = out.rearrange("s (c p) d -> p s c d", p=P)
        block = ctx.enter_context(nc.Block())

        @block.sync
        def _(eng):
            def load(name, dst, src):
                eng.dma_start(dst, src).then_inc(sem(name), 16)

            load("x0_in", x[:, 0], x_dram[:, 0])
            load("con_in", con[:], ins["consts"])
            load("wqk_in", wqk[:], ins["wqk"].rearrange("f p n -> p f n"))
            load("wvg_in", wv[:], ins["wv"])
            load("wvg_in", wg[:], ins["wg"])
            load("wo_in", wo[:], ins["wo"].rearrange("(t p) n -> p t n", p=P))
            for i in range(1, NSEQ):
                load(f"x{i}_in", x[:, i], x_dram[:, i])
                if i == 1:
                    load("wb_in", wqkv[:], ins["wqkv"])
                    load("wb_in", wproj[:], ins["wproj"])
                    load("wb_in", wrouter[:], ins["wrouter"])
                    load("wb_in", lnp[:], ins["lnp"])
                    load("rcon_in", rcon[:], ins["rconsts"])
                    load("w1_in", w1[:], ins["w1"].rearrange("e p n -> p e n"))
                    load("w2_in", w2[:], ins["w2"].rearrange("e (t p) n -> p e t n", p=P))
            for i in range(NSEQ):
                eng.wait_ge(sem("acc"), NC * NE * (i + 1))
                eng.dma_start(out_dram[:, i], res[:, i % 2]).then_inc(sem(f"stored{i % 2}"), 16)
            eng.wait_ge(sem("stored0"), 16 * NSEQ // 2)
            eng.wait_ge(sem("stored1"), 16 * NSEQ // 2)

        @block.gpsimd
        def _(eng):
            eng.memset(cum[:, 0, :], 0.0).then_inc(sem("cum0"), 1)
            eng.wait_ge(sem("con_in"), 16)

            def a_qx(i):
                eng.wait_ge(sem("rotated"), i + 1)
                if i >= 1:
                    eng.wait_ge(sem("scores"), 4 * i)
                for c in (1, 0):
                    for g in range(2):
                        hs = slice(4 * g, 4 * g + 4)
                        eng.tensor_tensor(
                            qx[:, c, hs, :],
                            qk[:, i % 2, 0, c * P:(c + 1) * P].unsqueeze(1).to_broadcast([P, 4, P]),
                            head_sel[:, hs].unsqueeze(2).to_broadcast([P, 4, P]),
                            ALU.mult).then_inc(sem("qx"), 1)

            def a_qkc(i):
                eng.wait_ge(sem("kc1"), i + 1)
                if i >= 1:
                    eng.wait_ge(sem("rowsum"), i)
                eng.tensor_tensor(qkc[:], qk[:, i % 2, 0], kcum[:], ALU.mult).then_inc(sem("qkc"), 1)

            def a_den(i):
                eng.wait_ge(sem("s2"), i + 1)
                if i >= 1:
                    eng.wait_ge(sem("tt"), i)
                eng.tensor_scalar(den[:], s2[:], 1.0, EPS, ALU.max, ALU.mult).then_inc(sem("den"), 1)

            def b_prodv(i):
                n = i + 1
                eng.wait_ge(sem("b_exp"), n)
                if i >= 1:
                    eng.wait_ge(sem("ao"), i)
                for c in range(NC):
                    eng.tensor_tensor(
                        prodv[:, c * n * D:(c + 1) * n * D].rearrange("p (a d) -> p a d", d=HD),
                        pe_[:, c * n * NH:(c + 1) * n * NH].unsqueeze(2).to_broadcast([P, n * NH, HD]),
                        v4[:, c, 0:n, :].rearrange("p t (h d) -> p (t h) d", d=HD),
                        ALU.mult).then_inc(sem("prodv"), 1)

            def b_base(i):
                eng.wait_ge(sem("h1"), i + 1)
                if i >= 2:
                    eng.wait_ge(sem("acc"), NC * (NE * (i - 2) + 1))
                eng.tensor_tensor(base[:, i % 2], h1[:], x1[:, i], ALU.add).then_inc(sem("base"), 1)

            follow({"a_qx": a_qx, "a_qkc": a_qkc, "a_den": a_den, "b_prodv": b_prodv, "b_base": b_base})

        @block.scalar
        def _(eng):
            table = [None]

            def use(name):
                if table[0] != name:
                    eng.preload_act_table_set(name)
                    table[0] = name

            def exp_ln():
                use("natural_log_exp_and_others")

            def copy(o, i_, name):
                eng.copy(o, i_).then_inc(sem(name), 1)

            def norm_scale(o, tmp, var, ready, n, name):
                exp_ln()
                eng.wait_ge(sem(ready), n)
                eng.activation(tmp, var, ACT.Ln).then_inc(sem(name + "_ln"), 1)
                eng.wait_ge(sem(name + "_ln"), n)
                eng.activation(o, tmp, ACT.Exp, scale=-0.5).then_inc(sem(name), 1)

            def a_norm(i):
                norm_scale(rstd[:, i % 2], lnv[:, i % 2], mv[:, i % 2, :, 1], "a_var", i + 1, "a_rstd")

            def a_xT(i):
                eng.wait_ge(sem("a_T"), i + 1)
                copy(xT[:, i % 2], g_ps[:, 0:SLEN], "xT")

            def a_gT(i):
                eng.wait_ge(sem("vg"), i + 1)
                if i >= 1:
                    eng.wait_ge(sem("og_raw"), i)
                copy(gT[:], g_ps[:], "gT")
                if i >= 1:
                    eng.wait_ge(sem("g_exp"), i)
                eng.activation(ag[:], g_ps[:], ACT.Abs).then_inc(sem("g_abs"), 1)

            def a_sigmoid(i):
                eng.wait_ge(sem("g_abs"), i + 1)
                exp_ln()
                eng.activation(ge[:], ag[:], ACT.Exp, scale=-1.0).then_inc(sem("g_exp"), 1)
                eng.wait_ge(sem("g_exp"), i + 1)
                if i >= 1:
                    eng.wait_ge(sem("g_log_sig"), i)
                eng.activation(gl[:], ge[:], ACT.Ln, bias=1.0).then_inc(sem("g_ln"), 1)

            def a_v(i):
                eng.wait_ge(sem("vg"), i + 1)
                if i >= 2:
                    eng.wait_ge(sem("x1"), i - 1)
                copy(v[:, i % 2], v_ps[:].rearrange("p (c n) -> p c n", c=NC), "v")

            def a_knat(i):
                eng.wait_ge(sem("kT"), i + 1)
                copy(knat[:], qks_ps[:, 0:P], "knat")

            def a_s2(i):
                eng.wait_ge(sem("rowsum"), i + 1)
                if i >= 1:
                    eng.wait_ge(sem("den"), i)
                eng.activation(s2[:], qk_ps[:], ACT.Square).then_inc(sem("s2"), 1)

            def a_osq(i):
                eng.wait_ge(sem("o"), i + 1)
                eng.activation(osq[:], qk_ps[:], ACT.Square).then_inc(sem("osq"), 1)

            def a_ln(i):
                exp_ln()
                eng.wait_ge(sem("tt"), i + 1)
                eng.activation(lt[:], tt[:], ACT.Ln).then_inc(sem("lt"), 1)

            def a_weight(i):
                exp_ln()
                eng.wait_ge(sem("z"), i + 1)
                eng.activation(wgt[:], z[:], ACT.Exp).then_inc(sem("wgt"), 1)

            def b_norm(i):
                norm_scale(br[:], bln[:], bv2[:], "b_var", i + 1, "b_rstd")

            def b_l1T(i):
                eng.wait_ge(sem("b_T"), i + 1)
                eng.wait_ge(sem("wb_in"), 64)
                eng.activation(l1T[:], b_ps[:, 0:SLEN], ACT.Identity, bias=lnp[:, 1:2],
                               scale=lnp[:, 0:1]).then_inc(sem("l1T"), 1)

            def b_kv(i):
                eng.wait_ge(sem("qkv"), i + 1)
                for c in range(NC):
                    for dst, off in ((k4, D), (v4, D + KVD)):
                        src = b_ps[:, c * 192 + off:c * 192 + off + KVD]
                        src = src.rearrange("p (g d) -> p g d", d=HD).unsqueeze(2)
                        copy(dst[:, c, i].rearrange("p (g r d) -> p g r d", g=NKV, r=QPK),
                             src.to_broadcast([P, NKV, QPK, HD]), "kv4")

            def b_exp(i):
                exp_ln()
                n = NC * (i + 1) * NH
                eng.wait_ge(sem("scm"), i + 1)
                if i >= 1:
                    eng.wait_ge(sem("prodv"), NC * i)
                    eng.wait_ge(sem("ssum"), i)
                eng.activation(pe_[:, 0:n], scm[:, 0:n], ACT.Exp, scale=HD ** -0.5).then_inc(sem("b_exp"), 1)

            def b_aoT(i):
                eng.wait_ge(sem("aoT_ps"), i + 1)
                copy(aoT[:], b_ps[:, 0:SLEN], "aoT")

            def c_norm(i):
                norm_scale(cr[:], cln[:], cv[:], "c_var", i + 1, "c_rstd")

            def c_x2T(i):
                eng.wait_ge(sem("c_T"), i + 1)
                eng.wait_ge(sem("wb_in"), 64)
                if i >= 2:
                    eng.wait_ge(sem("fc1"), NE * (i - 1))
                eng.activation(x2T[:, i % 2], b_ps[:, 0:SLEN], ACT.Identity, bias=lnp[:, 3:4],
                               scale=lnp[:, 2:3]).then_inc(sem("x2T"), 1)

            def c_exp(i):
                exp_ln()
                eng.wait_ge(sem("lsub"), i + 1)
                eng.activation(pr[:], lsub[:], ACT.Exp).then_inc(sem("pr"), 1)

            def m_gelu(i, e):
                n = NE * i + e
                use("gelu_apprx_tanh_and_others")
                eng.wait_ge(sem("fc1"), n + 1)
                if n >= 2:
                    eng.wait_ge(sem("fc2"), n - 1)
                eng.activation(hT[:, n % 2], fc1_ps[n % 2][:].rearrange("p (t n) -> p t n", t=NF),
                               ACT.Gelu_apprx_tanh).then_inc(sem("gelu"), 1)

            stages = {
                "a_rstd": a_norm, "a_xT": a_xT, "a_v": a_v, "a_gT": a_gT, "a_sigmoid": a_sigmoid,
                "a_knat": a_knat, "a_s2": a_s2, "a_osq": a_osq, "a_ln": a_ln, "a_weight": a_weight,
                "b_rstd": b_norm, "b_l1T": b_l1T, "b_kv4": b_kv, "b_exp": b_exp, "b_aoT": b_aoT,
                "c_rstd": c_norm, "c_x2T": c_x2T, "c_exp": c_exp,
            }
            for e in range(NE):
                stages[f"m_gelu_{e}"] = lambda i, e=e: m_gelu(i, e)
            follow(stages)

        @block.tensor
        def _(eng):
            mm = eng.matmul

            def a_T(i):
                eng.wait_ge(sem("a_xh"), NC * (i + 1))
                if i == 0:
                    eng.wait_ge(sem("con_in"), 16)
                if i >= 1:
                    eng.wait_ge(sem("sm"), 4 * i)
                for c in range(NC):
                    last = eng.transpose(g_ps[:, c * P:(c + 1) * P], xh[:, i % 2, c], ident)
                last.then_inc(sem("a_T"), 1)

            def a_qk(i):
                eng.wait_ge(sem("xT"), i + 1)
                t = xT[:, i % 2]
                if i == 0:
                    eng.wait_ge(sem("wqk_in"), 16)
                if i >= 1:
                    eng.wait_ge(sem("og_raw"), i)
                    eng.wait_ge(sem("tt"), i)
                for f in range(4):
                    last = mm(ps[f // 2][:, (f % 2) * SLEN:(f % 2 + 1) * SLEN], wqk[:, f], t,
                              start=True, stop=True)
                last.then_inc(sem("qk"), 1)

            def a_vg(i):
                t = xT[:, i % 2]
                if i == 0:
                    eng.wait_ge(sem("wvg_in"), 32)
                if i >= 1:
                    eng.wait_ge(sem("x1"), i)
                for c in range(NC):
                    mm(v_ps[:, c * VD:(c + 1) * VD], t[:, c * P:(c + 1) * P], wv[:], start=True, stop=True)
                for u in range(2):
                    last = mm(g_ps[:, u * SLEN:(u + 1) * SLEN], wg[:, u * P:(u + 1) * P], t,
                              start=True, stop=True)
                last.then_inc(sem("vg"), 1)

            def a_kT(i):
                eng.wait_ge(sem("rotated"), i + 1)
                eng.transpose(qks_ps[:, 0:P], qk[:, i % 2, 1, 0:P], ident).then_inc(sem("kT"), 1)

            def a_rowsums(i):
                eng.wait_ge(sem("qkc"), i + 1)
                for u in range(2):
                    last = mm(qk_ps[:, u * SLEN:(u + 1) * SLEN], same_head[:, u * P:(u + 1) * P], qkc[:],
                              start=True, stop=True)
                last.then_inc(sem("rowsum"), 1)

            def a_state_mm(i):
                eng.wait_ge(sem("knat"), i + 1)
                eng.wait_ge(sem("v"), i + 1)
                mm(qks_ps[:, P:P + VD], knat[:], v[:, i % 2, 0], start=True, stop=True).then_inc(sem("state_ps"), 1)

            def a_scores(i):
                for n, (c, g) in enumerate([(1, 0), (1, 1), (0, 0), (0, 1)]):
                    if n == 0:
                        eng.wait_ge(sem("v"), i + 1)
                        eng.wait_ge(sem("g_abs"), i + 1)
                    if n == 2:
                        eng.wait_ge(sem("s2"), i + 1)
                        eng.wait_ge(sem("state"), i + 1)
                    eng.wait_ge(sem("qx"), 4 * i + n + 1)
                    mm(ps[2 * c + g][:], qk[:, i % 2, 1, c * P:(c + 1) * P],
                       qx[:, c, 4 * g:4 * g + 4, :], start=True, stop=True).then_inc(sem("scores"), 1)

            def a_out(i):
                eng.wait_ge(sem("sm"), 4 * (i + 1))
                for u in range(2):
                    mm(qk_ps[:, u * SLEN + P:(u + 1) * SLEN], state[:, u * P:(u + 1) * P],
                       qk[:, i % 2, 0, P:SLEN], start=(u == 0), stop=False, skip_group_check=True)
                for c in range(NC):
                    for h in range(RH):
                        u, r = h // 4, h % 4
                        last = mm(qk_ps[32 * r:32 * r + 32, u * SLEN + c * P:u * SLEN + (c + 1) * P],
                                  v[:, i % 2, c, h * RV:(h + 1) * RV], sm[:, c, h, :],
                                  start=False, stop=(c == NC - 1 and u == 1), skip_group_check=True)
                last.then_inc(sem("o"), 1)

            def a_ms(i):
                eng.wait_ge(sem("osq"), i + 1)
                mm(qks_ps[:], head_mean, osq[:], start=True, stop=True).then_inc(sem("ms"), 1)

            def a_wo(i):
                eng.wait_ge(sem("og"), i + 1)
                if i == 0:
                    eng.wait_ge(sem("wo_in"), 16)
                for c in range(NC):
                    for u in range(2):
                        last = mm(v_ps[:, c * D:(c + 1) * D], og[:, u * SLEN + c * P:u * SLEN + (c + 1) * P],
                                  wo[:, u], start=(u == 0), stop=(u == 1))
                last.then_inc(sem("wo"), 1)

            def b_T(i):
                eng.wait_ge(sem("b_core"), NC * (i + 1))
                if i >= 1:
                    eng.wait_ge(sem("gate"), i)
                for c in range(NC):
                    last = eng.transpose(b_ps[:, c * P:(c + 1) * P], core[:, c], ident)
                last.then_inc(sem("b_T"), 1)

            def b_qkv(i):
                eng.wait_ge(sem("l1T"), i + 1)
                for c in range(NC):
                    last = mm(b_ps[:, c * 192:(c + 1) * 192], l1T[:, c * P:(c + 1) * P], wqkv[:],
                              start=True, stop=True)
                last.then_inc(sem("qkv"), 1)

            def b_aoT(i):
                eng.wait_ge(sem("aon"), i + 1)
                for c in range(NC):
                    last = eng.transpose(b_ps[:, c * P:(c + 1) * P], aon[:, c], ident)
                last.then_inc(sem("aoT_ps"), 1)

            def b_proj(i):
                eng.wait_ge(sem("aoT"), i + 1)
                for c in range(NC):
                    last = mm(b_ps[:, SLEN + c * P:SLEN + (c + 1) * P], aoT[:, c * P:(c + 1) * P], wproj[:],
                              start=True, stop=True)
                last.then_inc(sem("proj"), 1)

            def c_T(i):
                eng.wait_ge(sem("core2"), NC * (i + 1))
                for c in range(NC):
                    last = eng.transpose(b_ps[:, c * P:(c + 1) * P], core2[:, c], ident)
                last.then_inc(sem("c_T"), 1)

            def c_router(i):
                eng.wait_ge(sem("x2T"), i + 1)
                for c in range(NC):
                    last = mm(b_ps[:, SLEN + c * NE:SLEN + (c + 1) * NE], x2T[:, i % 2, c * P:(c + 1) * P],
                              wrouter[:], start=True, stop=True)
                last.then_inc(sem("logits"), 1)

            def c_rank(i):
                eng.wait_ge(sem("cum"), NC * (i + 1))
                for c in range(NC):
                    o = b_ps[:, SLEN + (NC + c) * NE:SLEN + (NC + c + 1) * NE]
                    mm(o, before[:, 0:P], selb[:, c], start=True, stop=False)
                    last = mm(o, before[:, P:], cum[:, NC * i + c, :], start=False, stop=True)
                last.then_inc(sem("rank"), 1)

            def m_fc1(i, e):
                n = NE * i + e
                if n >= 2:
                    eng.wait_ge(sem("gelu"), n - 1)
                if n == 0:
                    eng.wait_ge(sem("w1_in"), 16)
                if e == 0:
                    eng.wait_ge(sem("x2T"), i + 1)
                for t in range(NF):
                    last = mm(fc1_ps[n % 2][:, t * SLEN:(t + 1) * SLEN], w1[:, e, t * P:(t + 1) * P],
                              x2T[:, i % 2], start=True, stop=True)
                last.then_inc(sem("fc1"), 1)

            def m_fc2(i, e):
                n = NE * i + e
                eng.wait_ge(sem("gelu"), n + 1)
                if n == 0:
                    eng.wait_ge(sem("w2_in"), 16)
                if n >= 1:
                    eng.wait_ge(sem("acc"), NC * n)
                for c in range(NC):
                    for t in range(NF):
                        last = mm(fc2_ps[:, (n % 2) * SLEN + c * D:(n % 2) * SLEN + (c + 1) * D],
                                  hT[:, n % 2, t, c * P:(c + 1) * P], w2[:, e, t],
                                  start=(t == 0), stop=(t == NF - 1))
                last.then_inc(sem("fc2"), 1)

            stages = {
                "a_T": a_T, "a_qk": a_qk, "a_vg": a_vg, "a_kT": a_kT, "a_rowsums": a_rowsums,
                "a_state_mm": a_state_mm, "a_scores": a_scores, "a_out": a_out, "a_ms": a_ms, "a_wo": a_wo,
                "b_T": b_T, "b_qkv": b_qkv, "b_aoT_mm": b_aoT, "b_proj": b_proj,
                "c_T": c_T, "c_logits": c_router, "c_rank": c_rank,
            }
            for e in range(NE):
                stages[f"m_fc1_{e}"] = lambda i, e=e: m_fc1(i, e)
                stages[f"m_fc2_{e}"] = lambda i, e=e: m_fc2(i, e)
            follow(stages)

        @block.vector
        def _(eng):
            count = {}

            def done(ins_, name):
                ins_.then_inc(sem(name), 1)
                count[name] = count.get(name, 0) + 1

            def after(*names):
                for name in names:
                    eng.wait_ge(sem(name), count[name])

            tt_, ts_ = eng.tensor_tensor, eng.tensor_scalar

            def moments(src, st, out_, name):
                for c in range(NC):
                    done(eng.bn_stats(st[:, c], src[:, c]), name + "_stat")
                after(name + "_stat")
                for c in range(NC):
                    done(eng.bn_aggr(out_[:, c], st[:, c]), name + "_aggr")
                after(name + "_aggr")

            def a_moments(i):
                eng.wait_ge(sem(f"x{i}_in"), 16)
                moments(x[:, i], stat[:, i % 2], mv[:, i % 2], "a")
                done(ts_(mv[:, i % 2, :, 1], mv[:, i % 2, :, 1], EPS, None, ALU.add), "a_var")

            def a_xh(i):
                eng.wait_ge(sem("a_rstd"), i + 1)
                for c in range(NC):
                    done(ts_(xh[:, i % 2, c], x[:, i, c], mv[:, i % 2, c, 0:1], rstd[:, i % 2, c:c + 1],
                             ALU.subtract, ALU.mult), "a_xh")

            def a_rotate(i):
                eng.wait_ge(sem("qk"), i + 1)
                done(tt_(rot_a[:], qk_ps[:], cos_t, ALU.mult), "rot_a")
                done(tt_(rot_b[:], qks_ps[:], sin_t, ALU.mult), "rot_b")
                after("rot_b")
                done(tt_(qk[:, i % 2].rearrange("p f n -> p (f n)"), rot_a[:], rot_b[:], ALU.add), "rotated")

            def a_kcum(i):
                after("rotated")
                if i >= 1:
                    eng.wait_ge(sem("qkc"), i)
                k = qk[:, i % 2, 1]
                done(eng.tensor_tensor_scan(kcum[:, 0:P], ones, k[:, 0:P], 0.0, ALU.mult, ALU.add), "kc0")
                after("kc0")
                done(tt_(kinit[:], kcum[:, P - 1:P], chunk_decay, ALU.mult), "kinit")
                after("kinit")
                done(eng.tensor_tensor_scan(kcum[:, P:SLEN], ones, k[:, P:SLEN], kinit[:], ALU.mult, ALU.add), "kc1")

            def a_log_sigmoid(i):
                eng.wait_ge(sem("g_ln"), i + 1)
                done(eng.scalar_tensor_tensor(gm[:], gT[:], 0.0, gl[:], ALU.min, ALU.subtract), "g_log_sig")

            def a_state(i):
                eng.wait_ge(sem("state_ps"), i + 1)
                done(tt_(state[:], qks_ps[:, P:P + VD], state_mask, ALU.mult), "state")

            def a_mask(i):
                for n, (c, g) in enumerate([(1, 0), (1, 1), (0, 0), (0, 1)]):
                    eng.wait_ge(sem("scores"), 4 * i + n + 1)
                    done(tt_(sm[:, c, 4 * g:4 * g + 4, :], ps[2 * c + g][:].rearrange("p (h n) -> p h n", h=4),
                             tri.unsqueeze(1).to_broadcast([P, 4, P]), ALU.mult), "sm")

            def a_scale_in(i):
                eng.wait_ge(sem("ms"), i + 1)
                eng.wait_ge(sem("den"), i + 1)
                done(tt_(tt[:], qks_ps[:], den[:], ALU.add), "tt")

            def a_z(i):
                eng.wait_ge(sem("lt"), i + 1)
                after("g_log_sig")
                done(eng.scalar_tensor_tensor(z[:], lt[:], -0.5, gm[:], ALU.mult, ALU.add), "z")

            def a_og_raw(i):
                eng.wait_ge(sem("osq"), i + 1)
                eng.wait_ge(sem("gT"), i + 1)
                done(tt_(og[:], qk_ps[:], gT[:], ALU.mult), "og_raw")

            def a_og(i):
                eng.wait_ge(sem("wgt"), i + 1)
                after("og_raw")
                done(tt_(og[:], og[:], wgt[:], ALU.mult), "og")

            def a_x1(i):
                eng.wait_ge(sem("wo"), i + 1)
                done(tt_(x1[:, i], v_ps[:, 0:SLEN].rearrange("p (c n) -> p c n", c=NC), x[:, i], ALU.add), "x1")

            def b_moments(i):
                after("x1")
                moments(x1[:, i], bstat, bmv, "b")
                done(ts_(bv2[:, :, 0], bmv[:, :, 1], EPS, None, ALU.add), "b_var0")
                done(ts_(bv2[:, :, 1], bmv[:, :, 1], 1.0 + EPS, EPS * EPS, ALU.mult, ALU.add), "b_var")

            def b_core(i):
                eng.wait_ge(sem("b_rstd"), i + 1)
                for c in range(NC):
                    done(ts_(core[:, c], x1[:, i, c], bmv[:, c, 0:1], br[:, c, 1:2],
                             ALU.subtract, ALU.mult), "b_core")
                for c in range(NC):
                    done(ts_(hid[:, c], x1[:, i, c], bmv[:, c, 0:1], br[:, c, 0:1],
                             ALU.subtract, ALU.mult), "hid")

            def b_scores(i):
                n = i + 1
                eng.wait_ge(sem("kv4"), 4 * n)
                q = b_ps[:, 0:2 * 192].rearrange("p (c n) -> p c n", c=NC)[:, :, 0:D]
                pv = prod[:, 0:NC * n * D]
                done(tt_(pv.rearrange("p (c t f) -> p c t f", c=NC, t=n),
                         q.unsqueeze(2).to_broadcast([P, NC, n, D]), k4[:, :, 0:n, :], ALU.mult), "prod")
                after("prod")
                done(eng.tensor_reduce(sc[:, 0:NC * n * NH], pv.rearrange("p (a d) -> p a d", d=HD), X, ALU.add), "sc")

            def b_scores2(i):
                n = i + 1
                after("sc")
                s = sc[:, 0:NC * n * NH].rearrange("p (c t h) -> p c t h", c=NC, t=n)
                done(eng.tensor_reduce(mx[:], s.rearrange("p c t h -> p c h t"), X, ALU.max), "mx")
                after("mx")
                done(tt_(scm[:, 0:NC * n * NH].rearrange("p (c t h) -> p c t h", c=NC, t=n), s,
                         mx[:].unsqueeze(2).to_broadcast([P, NC, n, NH]), ALU.subtract), "scm")

            def b_sum(i):
                n = i + 1
                eng.wait_ge(sem("b_exp"), n)
                e = pe_[:, 0:NC * n * NH]
                done(eng.tensor_reduce(ssum[:], e.rearrange("p (c t h) -> p c h t", c=NC, t=n), X, ALU.add), "ssum")
                after("ssum")
                done(eng.reciprocal(rsum[:], ssum[:]), "rsum")

            def b_ao(i):
                n = i + 1
                eng.wait_ge(sem("prodv"), NC * n)
                pv = prodv[:, 0:NC * n * D]
                done(eng.tensor_reduce(ao[:], pv.rearrange("p (c t f) -> p c f t", c=NC, t=n), X, ALU.add), "ao")

            def b_norm(i):
                after("ao", "rsum")
                done(tt_(aon[:].rearrange("p c (h d) -> p (c h) d", d=HD),
                         ao[:].rearrange("p c (h d) -> p (c h) d", d=HD),
                         rsum[:].rearrange("p c h -> p (c h)").unsqueeze(2).to_broadcast([P, NC * NH, HD]),
                         ALU.mult), "aon")

            def c_h1(i):
                eng.wait_ge(sem("proj"), i + 1)
                after("hid")
                done(tt_(h1[:], b_ps[:, SLEN:2 * SLEN].rearrange("p (c n) -> p c n", c=NC), hid[:], ALU.add), "h1")

            def c_moments(i):
                after("h1")
                moments(h1, cstat, cmv, "c")
                done(ts_(cv[:], cmv[:, :, 1], EPS, None, ALU.add), "c_var")

            def c_core(i):
                eng.wait_ge(sem("c_rstd"), i + 1)
                for c in range(NC):
                    done(ts_(core2[:, c], h1[:, c], cmv[:, c, 0:1], cr[:, c:c + 1],
                             ALU.subtract, ALU.mult), "core2")

            def c_lsub(i):
                eng.wait_ge(sem("logits"), i + 1)
                lg = b_ps[:, SLEN:SLEN + NC * NE].rearrange("p (c e) -> p c e", c=NC)
                done(eng.tensor_reduce(lmx[:], lg, X, ALU.max), "lmx")
                after("lmx")
                done(tt_(lsub[:], lg, lmx[:].unsqueeze(2).to_broadcast([P, NC, NE]), ALU.subtract), "lsub")

            def c_place(i):
                if i == 0:
                    eng.wait_ge(sem("rcon_in"), 16)
                    done(eng.tensor_copy(before[:], rcon[:, 0:2 * P]), "before")
                    eng.wait_ge(sem("cum0"), 1)
                eng.wait_ge(sem("pr"), i + 1)
                low = lower.rearrange("p (e j) -> p e j", e=NE)
                for c in range(NC):
                    mine = pr[:, c].unsqueeze(2).to_broadcast([P, NE, NE])
                    other = pr[:, c].unsqueeze(1).to_broadcast([P, NE, NE])
                    done(tt_(cgt[:, c], other, mine, ALU.is_gt), "cgt")
                    done(tt_(cge[:, c], other, mine, ALU.is_ge), "cge")
                after("cge")
                done(tt_(cgl[:], cge[:], low.unsqueeze(1).to_broadcast([P, NC, NE, NE]), ALU.mult), "cgl")
                after("cgl")
                done(tt_(cor[:], cgl[:], cgt[:], ALU.max), "cor")
                after("cor")
                done(eng.tensor_reduce(place[:], cor[:], X, ALU.add), "place")

            def c_select(i):
                after("place")
                done(ts_(selb[:], place[:], TOPK - 0.5, None, ALU.is_lt), "selb")
                done(ts_(sel[:], place[:], TOPK - 0.5, None, ALU.is_lt), "sel")
                after("sel")
                for c in range(NC):
                    n = NC * i + c
                    done(tt_(cum[:, n + 1, :], cum[:, n, :], selb[:, c], ALU.add), "cum")
                    after("cum")

            def c_gsel(i):
                after("sel")
                done(tt_(chosen[:], pr[:], sel[:], ALU.mult), "chosen")
                after("chosen")
                done(eng.tensor_reduce(csum[:], chosen[:], X, ALU.add), "csum")
                after("csum")
                done(eng.reciprocal(crec[:], csum[:]), "crec")
                after("crec")
                done(tt_(gsel[:], chosen[:], crec[:].unsqueeze(2).to_broadcast([P, NC, NE]), ALU.mult), "gsel")

            def c_gate(i):
                eng.wait_ge(sem("rank"), i + 1)
                rk = b_ps[:, SLEN + NC * NE:SLEN + 2 * NC * NE].rearrange("p (c e) -> p c e", c=NC)
                done(ts_(fits[:], rk, CAP - 0.5, None, ALU.is_lt), "fits")
                after("fits", "gsel")
                done(tt_(gate[:, i % 2], gsel[:], fits[:], ALU.mult), "gate")

            def m_acc(i, e):
                n = NE * i + e
                eng.wait_ge(sem("fc2"), n + 1)
                if e == 0:
                    after("gate")
                    eng.wait_ge(sem("base"), i + 1)
                else:
                    after("acc")
                if e == NE - 1 and i >= 2:
                    eng.wait_ge(sem(f"stored{i % 2}"), 16 * (i // 2))
                for c in range(NC):
                    o = fc2_ps[:, (n % 2) * SLEN + c * D:(n % 2) * SLEN + (c + 1) * D]
                    prev = base[:, i % 2, c] if e == 0 else acc[:, i % 2, (e - 1) % 2, c]
                    dst = res[:, i % 2, c] if e == NE - 1 else acc[:, i % 2, e % 2, c]
                    done(eng.scalar_tensor_tensor(dst, o, gate[:, i % 2, c, e:e + 1], prev,
                                                  ALU.mult, ALU.add), "acc")

            eng.wait_ge(sem("con_in"), 16)
            stages = {
                "a_moments": a_moments, "a_xh": a_xh, "a_rotate": a_rotate, "a_kcum": a_kcum,
                "a_log_sigmoid": a_log_sigmoid, "a_state": a_state, "a_mask": a_mask,
                "a_scale_in": a_scale_in, "a_z": a_z, "a_og_raw": a_og_raw, "a_og": a_og, "a_x1": a_x1,
                "b_moments": b_moments, "b_core": b_core, "b_scores": b_scores, "b_scores2": b_scores2,
                "b_sum": b_sum, "b_ao": b_ao, "b_norm": b_norm, "b_h1": c_h1,
                "c_moments": c_moments, "c_core": c_core, "c_lsub": c_lsub, "c_place": c_place,
                "c_select": c_select, "c_gsel": c_gsel, "c_gate": c_gate,
            }
            for e in range(NE):
                stages[f"m_acc_{e}"] = lambda i, e=e: m_acc(i, e)
            follow(stages)


def lay_out(a):
    f = lambda n: np.ascontiguousarray(np.asarray(a[n]))
    wq, wk = f("L0_attn_wq"), f("L0_attn_wk")
    swap = np.arange(D) ^ 1
    per = f("L0_ffn_qkv_weight").reshape(NKV, (QPK + 2) * HD, D)
    q, k, v = per[:, :QPK * HD], per[:, QPK * HD:(QPK + 1) * HD], per[:, (QPK + 1) * HD:]
    return {
        "x": f("L0_attn_x"),
        "consts": retention_constants(),
        "rconsts": routing_constants(),
        "wqk": np.stack([wq, wk, wq[:, swap], wk[:, swap]]),
        "wv": f("L0_attn_wv"), "wg": f("L0_attn_wg"), "wo": f("L0_attn_wo"),
        "wqkv": np.concatenate([t.reshape(-1, D) for t in (q, k, v)]).T,
        "wproj": f("L0_ffn_proj_weight").T,
        "wrouter": f("L0_ffn_router_weight"),
        "lnp": np.stack([f("L0_ffn_ln1_weight"), f("L0_ffn_ln1_bias"), f("L0_ffn_ln2_weight"), f("L0_ffn_ln2_bias")], 1),
        "w1": f("L0_ffn_moe_w1"), "w2": f("L0_ffn_moe_w2"),
    }


def kernel(**inputs):
    import concourse.bacc as _bacc
    from concourse.bass_utils import run_bass_kernel_spmd as _run

    nc = _bacc.Bacc("TRN2", target_bir_lowering=False, num_devices=1)
    arrays = {f"in_{n}": np.ascontiguousarray(a) for n, a in lay_out(inputs).items()}
    ins = {n[3:]: nc.dram_tensor(n, a.shape, mybir.dt.from_np(a.dtype), kind="ExternalInput").ap()
           for n, a in arrays.items()}
    out = nc.dram_tensor("out", (NSEQ, SLEN, D), F32, kind="ExternalOutput").ap()
    build(nc, ins, out)
    r = _run(nc, [arrays], core_ids=[0])
    return r.results[0]["out"]
```

```python
from contextlib import ExitStack

import numpy as np

import concourse.bass as bass
from concourse import mybir

ALU = mybir.AluOpType
ACT = mybir.ActivationFunctionType
F32 = mybir.dt.float32
BF16 = mybir.dt.bfloat16
X = mybir.AxisListType.X

P = 128
NSEQ = 8
SLEN = 256
NC = SLEN // P
D = 128
VD = 256
RH = 8
RK = D // RH
RV = VD // RH
NH, NKV = 16, 4
QPK = NH // NKV
HD = D // NH
KVD = NKV * HD
NE = 8
F = 256
NF = F // P
TOPK = 2
CAP = -(-NSEQ * SLEN * TOPK * 5 // (NE * 4))
EPS = 1e-5


ORDER = """
a_osq@1 a_den@1 m_fc1_4@1 a_ms@1 b_sum@1 b_ao@1 m_acc_2@1 b_norm@1 m_fc2_3@1 a_scale_in@1 m_gelu_4@1
a_og_raw@1 b_aoT_mm@1 a_ln@1 b_aoT@1 a_log_sigmoid@1 m_acc_3@1 b_hid@1 b_proj@1 a_z@1 b_h1@1
c_stats@1 a_weight@1 b_base@1 c_moments@1 c_var@1 c_rstd@1 m_fc2_4@1 a_og@1 m_fc1_5@1 a_stats
m_acc_4@1 c_core@1 m_fc1_6@1 m_gelu_5@1 a_wo@1 c_T@1 a_x1@1 m_fc2_5@1 b_stats m_gelu_6@1 c_x2T@1
a_moments c_logits@1 b_moments m_fc1_7@1 m_acc_5@1 a_var b_var c_lsub@1 m_fc2_6@1 a_rstd c_exp@1
m_fc1_0 c_place@1 a_xh b_rstd a_T c_ties@1 a_xT a_qk c_or@1 m_acc_6@1 m_gelu_7@1 c_count@1
c_select@1 c_chosen@1 c_sum@1 b_core c_rec@1 a_rotate a_vg c_gsel@1 c_rank@1 m_gelu_0 a_rotated a_v
m_fc2_7@1 c_gate@1 b_T b_l1T m_fc1_1 m_acc_7@1 a_kT b_qkv a_kcum a_knat m_fc2_0 m_acc_0 b_kv4 a_gT
a_qkc a_rowsums m_fc1_2 b_prod b_scores a_state_mm m_gelu_1 m_gelu_2 m_fc2_1 b_scores2 a_qx m_fc1_3
a_state a_s2 a_scores m_acc_1 b_exp a_mask m_fc2_2 a_out b_prodv a_sigmoid m_gelu_3
""".split()
LAG = {"a": 0, "b": 1, "c": 1, "m": 2}

FIRST = """
a_stats:0 a_moments:0 a_var:0 a_rstd:0 a_xh:0 a_T:0 a_xT:0 a_qk:0 a_rotate:0 a_rotated:0 a_kcum:0
a_vg:0 a_stats:1 a_qkc:0 a_kT:0 a_qx:0 a_v:0 a_knat:0 a_gT:0 a_state_mm:0 a_sigmoid:0 a_rowsums:0
a_moments:1 a_s2:0 a_state:0 a_scores:0 a_var:1 a_rstd:1 a_mask:0 a_out:0 a_osq:0 a_log_sigmoid:0
a_den:0 a_og_raw:0 a_ms:0 a_scale_in:0 a_ln:0 a_xh:1 a_z:0 a_T:1 a_weight:0 a_stats:2 a_og:0 a_wo:0
a_xT:1 a_x1:0 b_stats:0 b_moments:0 b_var:0 a_qk:1 b_rstd:0 a_rotate:1 a_rotated:1 b_core:0 a_vg:1
a_kcum:1 b_T:0 a_kT:1 a_moments:2 a_var:2 a_gT:1 a_qx:1 b_l1T:0 b_qkv:0 a_v:1 a_knat:1 a_qkc:1
a_state_mm:1 b_kv4:0 a_rowsums:1 a_s2:1 b_prod:0 b_hid:0 a_state:1 b_scores:0 a_den:1 a_rstd:2
b_scores2:0 a_sigmoid:1 a_scores:1 b_exp:0 a_mask:1 b_sum:0 a_out:1 b_prodv:0 b_ao:0 b_norm:0
b_aoT_mm:0 b_aoT:0 a_osq:1 a_log_sigmoid:1 b_proj:0 b_h1:0 a_ms:1 c_stats:0 a_xh:2 a_scale_in:1
a_ln:1 c_moments:0 a_og_raw:1 c_var:0 a_T:2 a_z:1 a_xT:2 a_qk:2 c_rstd:0 c_core:0 c_T:0 a_weight:1
c_x2T:0 a_og:1 c_logits:0 a_rotate:2 a_wo:1 b_base:0 m_fc1_0:0 c_lsub:0 a_vg:2 a_x1:1 c_exp:0
b_stats:1 c_place:0 b_moments:1 c_ties:0 b_var:1 c_or:0 c_count:0 b_rstd:1 b_hid:1 b_core:1
a_rotated:2 c_select:0 c_rank:0 m_gelu_0:0 m_fc1_1:0 c_chosen:0 b_T:1 c_sum:0 c_rec:0 b_l1T:1
c_gsel:0 a_gT:2 c_gate:0 a_kcum:2 m_fc2_0:0 a_qkc:2 b_qkv:1 a_rowsums:2 m_acc_0:0 b_kv4:1 a_kT:2
m_fc1_2:0 b_prod:1 m_gelu_1:0 a_v:2 m_fc2_1:0 m_fc1_3:0 b_scores:1 a_knat:2 a_s2:2 a_state_mm:2
b_scores2:1 a_state:2 m_gelu_2:0 b_exp:1 m_acc_1:0 a_qx:2 a_scores:2 a_sigmoid:2 b_prodv:1 a_den:2
b_sum:1 m_fc2_2:0 a_mask:2 b_ao:1 a_out:2 m_fc1_4:0 a_log_sigmoid:2 m_gelu_3:0 m_acc_2:0 b_norm:1
a_osq:2 b_aoT_mm:1 m_gelu_4:0 a_og_raw:2 b_aoT:1 a_stats:3 a_ms:2 m_fc2_3:0 b_proj:1 a_scale_in:2
m_fc1_5:0 m_acc_3:0 a_ln:2 b_h1:1 a_z:2 m_fc2_4:0 c_stats:1 c_moments:1 m_fc1_6:0 c_var:1 a_weight:2
a_og:2 a_wo:2
""".split()
LAST = """
m_gelu_6:4 a_x1:6 c_T:5 c_x2T:5 m_fc2_5:4 b_base:5 b_stats:6 c_logits:5 a_moments:7 b_moments:6
m_acc_5:4 c_lsub:5 b_var:6 c_exp:5 m_fc1_7:4 a_var:7 a_rstd:7 a_xh:7 m_fc2_6:4 a_T:7 m_fc1_0:5
c_place:5 c_ties:5 b_rstd:6 b_hid:6 c_or:5 m_acc_6:4 c_count:5 m_gelu_7:4 c_select:5 a_xT:7
c_chosen:5 c_rank:5 a_qk:7 b_core:6 c_sum:5 c_rec:5 c_gsel:5 m_gelu_0:5 m_fc2_7:4 b_T:6 c_gate:5
a_rotate:7 a_vg:7 b_l1T:6 b_qkv:6 m_fc2_0:5 a_gT:7 m_fc1_1:5 a_rotated:7 m_acc_7:4 a_kT:7 a_kcum:7
m_fc1_2:5 b_kv4:6 a_knat:7 a_qkc:7 a_rowsums:7 b_prod:6 a_qx:7 m_gelu_1:5 m_acc_0:5 b_scores:6 a_v:7
a_s2:7 a_state_mm:7 b_scores2:6 b_exp:6 a_sigmoid:7 a_state:7 b_prodv:6 m_gelu_2:5 m_fc2_1:5
m_acc_1:5 a_scores:7 a_mask:7 b_sum:6 b_ao:6 m_fc1_3:5 m_fc2_2:5 m_acc_2:5 a_den:7 m_gelu_3:5
a_out:7 a_osq:7 m_fc1_4:5 a_ms:7 b_norm:6 a_scale_in:7 m_fc2_3:5 m_gelu_4:5 b_aoT_mm:6 a_ln:7
m_fc1_5:5 a_og_raw:7 b_aoT:6 a_log_sigmoid:7 m_acc_3:5 a_z:7 b_proj:6 b_h1:6 c_stats:6 m_fc2_4:5
c_moments:6 c_var:6 a_weight:7 a_og:7 m_fc1_6:5 c_rstd:6 c_core:6 m_acc_4:5 a_wo:7 m_gelu_5:5
m_gelu_6:5 c_T:6 c_x2T:6 a_x1:7 b_stats:7 b_moments:7 m_fc2_5:5 c_logits:6 b_var:7 m_acc_5:5
c_lsub:6 m_fc1_7:5 c_exp:6 b_rstd:7 m_gelu_7:5 m_fc2_6:5 c_place:6 b_core:7 m_fc1_0:6 m_acc_6:5
c_ties:6 c_or:6 c_count:6 c_select:6 b_T:7 m_fc2_7:5 c_chosen:6 c_rank:6 m_gelu_0:6 m_acc_7:5
b_l1T:7 c_sum:6 b_qkv:7 b_base:6 b_kv4:7 c_rec:6 m_fc2_0:6 c_gsel:6 c_gate:6 m_fc1_1:6 m_gelu_1:6
m_acc_0:6 b_hid:7 m_fc1_2:6 b_prod:7 m_gelu_2:6 b_scores:7 m_fc1_3:6 b_scores2:7 m_fc2_1:6 b_exp:7
m_acc_1:6 b_sum:7 m_fc1_4:6 m_gelu_3:6 m_fc2_2:6 b_prodv:7 m_acc_2:6 m_fc1_5:6 b_ao:7 m_fc2_3:6
b_norm:7 b_aoT_mm:7 m_acc_3:6 b_aoT:7 b_proj:7 b_h1:7 m_gelu_4:6 c_stats:7 c_moments:7 m_fc2_4:6
m_gelu_5:6 m_fc1_6:6 c_var:7 c_rstd:7 m_acc_4:6 m_fc2_5:6 c_core:7 m_gelu_6:6 m_acc_5:6 c_T:7
c_x2T:7 c_logits:7 c_lsub:7 c_exp:7 m_fc2_6:6 c_place:7 c_ties:7 m_fc1_7:6 m_fc1_0:7 m_acc_6:6
m_gelu_7:6 c_or:7 m_fc2_7:6 c_count:7 c_select:7 c_chosen:7 m_acc_7:6 c_rank:7 m_fc1_1:7 c_sum:7
m_gelu_0:7 b_base:7 m_fc2_0:7 c_rec:7 m_gelu_1:7 c_gsel:7 c_gate:7 m_fc1_2:7 m_gelu_2:7 m_acc_0:7
m_fc2_1:7 m_acc_1:7 m_fc1_3:7 m_fc2_2:7 m_gelu_3:7 m_fc1_4:7 m_acc_2:7 m_fc2_3:7 m_gelu_4:7
m_fc1_5:7 m_acc_3:7 m_fc2_4:7 m_gelu_5:7 m_fc1_6:7 m_gelu_6:7 m_acc_4:7 m_fc2_5:7 m_fc1_7:7
m_gelu_7:7 m_acc_5:7 m_fc2_6:7 m_acc_6:7 m_fc2_7:7 m_acc_7:7
""".split()


def follow(stages):
    def run(irregular):
        for name, _, i in (x.partition(":") for x in irregular):
            if name in stages:
                stages[name](int(i))

    run(FIRST)
    elsewhere = set(FIRST + LAST)
    order = [(name, LAG[name[0]] + int(late or 0)) for name, _, late in (x.partition("@") for x in ORDER)]
    for step in range(NSEQ + 1 + max(lag for _, lag in order)):
        for name, lag in order:
            i = step - lag
            if name in stages and 0 <= i < NSEQ and f"{name}:{i}" not in elsewhere:
                stages[name](i)
    run(LAST)


def pool_tiles(i, split_from):
    return range(NC) if i < split_from else range(1, NC)


PROD_SPLIT, PRODV_SPLIT = 3, 4
VECTOR_FIRST = 2


def retention_constants():
    lin = np.linspace(0.0, 1.0, RK // 2).astype(np.float32)
    angle = np.repeat((1.0 / np.float32(10000.0) ** lin).astype(np.float32), 2)
    decay = np.log1p(-2.0 ** (-5.0 - np.arange(RH)))
    idx = np.arange(SLEN)
    phase = (idx[:, None].astype(np.float32) * angle[None, :]).astype(np.float32).astype(np.float64)
    sin, cos = np.sin(phase), np.cos(phase)
    diff = idx[:, None] - idx[None, :]
    rows = np.stack([np.where(diff >= 0, np.exp(np.minimum(diff * -1.0, 0) * -decay[h]), 0).sum(-1)
                     for h in range(RH)])
    local = idx % P
    sign = np.where(np.arange(RK) % 2 == 0, -1.0, 1.0)
    fq = np.exp(local[None] * decay[:, None]) / np.sqrt(rows)
    fk = np.exp(-local[None] * decay[:, None]) * RK ** -0.5
    feat = lambda f, w: (f[:, None, :] * w.T[None]).reshape(D, SLEN)
    cos_t = np.concatenate([feat(fq, cos), feat(fk, cos)], 1)
    sin_t = np.concatenate([feat(fq, sin * sign), feat(fk, sin * sign)], 1)
    head_k, head_v = np.arange(D) // RK, np.arange(VD) // RV
    chunk_decay = np.exp(P * decay)[head_k][:, None]
    same = head_k[:, None] == head_v[None]
    parts = [np.eye(P), cos_t, sin_t, same * chunk_decay, same * 1.0,
             ((np.arange(P) // RV)[:, None] == (np.arange(P) // RV)[None]) * (1.0 / RV),
             np.arange(P)[:, None] <= np.arange(P)[None],
             head_k[:, None] == np.arange(RH)[None], chunk_decay, np.ones((P, P))]
    return np.concatenate([np.asarray(p, np.float32) for p in parts], 1)


def routing_constants():
    lower = (np.arange(NE)[None] < np.arange(NE)[:, None]).reshape(1, NE * NE)
    return np.concatenate([np.arange(P)[:, None] < np.arange(P)[None], np.ones((P, P)),
                           np.repeat(lower, P, 0)], 1).astype(np.float32)


def build(nc, ins, out):
    ctx = ExitStack()
    with ctx:
        def sb(name, shape, dt=F32):
            return ctx.enter_context(nc.sbuf_tensor(name, shape, dt))

        class Signals:
            def __init__(self):
                self.made = {}

            def __call__(self, name):
                if name not in self.made:
                    self.made[name] = ctx.enter_context(nc.semaphore(name))
                return self.made[name]

        sem = Signals()

        wqk = sb("wqk", [P, 2, D])
        wv = sb("wv", [P, VD])
        wg = sb("wg", [P, VD])
        wo = sb("wo", [P, 2, D])
        wqkv = sb("wqkv", [P, D + 2 * KVD])
        wproj = sb("wproj", [P, D])
        wrouter = sb("wrouter", [P, NE])
        w1 = sb("w1", [P, NE, F])
        w2 = sb("w2", [P, NE, NF, D])
        lnp = sb("lnp", [P, 4])
        NCONST = ins["consts"].shape[1]
        con = sb("con", [P, NCONST])
        at = [0]

        def part(n):
            at[0] += n
            return con[:, at[0] - n:at[0]]

        ident = part(P)
        cos_t, sin_t = part(2 * SLEN), part(2 * SLEN)
        state_mask, same_head, head_mean, tri = part(VD), part(VD), part(P), part(P)
        head_sel, chunk_decay, ones = part(RH), part(1), part(P)
        rcon = sb("rcon", [P, 2 * P + NE * NE])
        before = sb("before", [P, 2 * P], BF16)
        lower = rcon[:, 2 * P:]

        x = sb("x", [P, NSEQ, NC, D])
        x1 = sb("x1", [P, NSEQ, NC, D])
        stat = sb("stat", [P, 2, NC, 6])
        mv = sb("mv", [P, 2, NC, 2])
        lnv = sb("lnv", [P, 2, NC])
        rstd = sb("rstd", [P, 2, NC])
        xh = sb("xh", [P, 2, NC, D])
        xT = sb("xT", [P, 2, SLEN])
        rot_a = sb("rot_a", [P, 2 * SLEN])
        swapped = sb("swapped", [P, 2 * SLEN])
        rot_b = sb("rot_b", [P, 2 * SLEN])
        qk = sb("qk", [P, 2, 2, SLEN])
        xh_sub = sb("xh_sub", [P, NC, D])
        hid_sub = sb("hid_sub", [P, NC, D])
        gneg = sb("gneg", [P, 2 * SLEN])
        q_sb = sb("q_sb", [P, NC, D])
        qx = sb("qx", [P, NC, RH, P])
        v = sb("v", [P, 2, NC, VD])
        ag = sb("ag", [P, 2 * SLEN])
        ge = sb("ge", [P, 2 * SLEN])
        gl = sb("gl", [P, 2 * SLEN])
        gm = sb("gm", [P, 2 * SLEN])
        gT = sb("gT", [P, 2 * SLEN])
        kcum = sb("kcum", [P, SLEN])
        kinit = sb("kinit", [P, 1])
        qkc = sb("qkc", [P, SLEN])
        s2 = sb("s2", [P, 2 * SLEN])
        den = sb("den", [P, 2 * SLEN])
        knat = sb("knat", [P, P])
        state = sb("state", [P, VD])
        sm = sb("sm", [P, NC, RH, P])
        osq = sb("osq", [P, 2 * SLEN])
        tt = sb("tt", [P, 2 * SLEN])
        lt = sb("lt", [P, 2 * SLEN])
        z = sb("z", [P, 2 * SLEN])
        wgt = sb("wgt", [P, 2 * SLEN])
        og = sb("og", [P, 2 * SLEN])

        bstat = sb("bstat", [P, NC, 6])
        bmv = sb("bmv", [P, NC, 2])
        bv2 = sb("bv2", [P, NC, 2])
        bln = sb("bln", [P, NC, 2])
        br = sb("br", [P, NC, 2])
        hid = sb("hid", [P, NC, D])
        core = sb("core", [P, NC, D])
        l1T = sb("l1T", [P, SLEN])
        k4 = sb("k4", [P, NC, NSEQ, D])
        v4 = sb("v4", [P, NC, NSEQ, D])
        prod = sb("prod", [P, NC * NSEQ * D])
        prodv = sb("prodv", [P, NC * NSEQ * D])
        sc = sb("sc", [P, NC * NSEQ * NH])
        scm = sb("scm", [P, NC * NSEQ * NH])
        attn_exp = sb("attn_exp", [P, NC * NSEQ * NH])
        mx = sb("mx", [P, NC, NH])
        ssum = sb("ssum", [P, NC, NH])
        rsum = sb("rsum", [P, NC, NH])
        ao = sb("ao", [P, NC, D])
        aon = sb("aon", [P, NC, D])
        aoT = sb("aoT", [P, SLEN])
        h1 = sb("h1", [P, NC, D])
        cstat = sb("cstat", [P, NC, 6])
        cmv = sb("cmv", [P, NC, 2])
        cv = sb("cv", [P, NC])
        cln = sb("cln", [P, NC])
        cr = sb("cr", [P, NC])
        core2 = sb("core2", [P, NC, D])
        x2T = sb("x2T", [P, 2, SLEN])
        lmx = sb("lmx", [P, NC])
        lsub = sb("lsub", [P, NC, NE])
        pr = sb("pr", [P, NC, NE])
        cgt = sb("cgt", [P, NC, NE, NE])
        cge = sb("cge", [P, NC, NE, NE])
        cgl = sb("cgl", [P, NC, NE, NE])
        cor = sb("cor", [P, NC, NE, NE])
        place = sb("place", [P, NC, NE])
        sel = sb("sel", [P, NC, NE])
        selb = sb("selb", [P, NC, NE], BF16)
        cum = sb("cum", [P, 2 * NSEQ + 1, NE], BF16)
        chosen = sb("chosen", [P, NC, NE])
        csum = sb("csum", [P, NC])
        crec = sb("crec", [P, NC])
        fits = sb("fits", [P, NC, NE])
        gsel = sb("gsel", [P, NC, NE])
        gate = sb("gate", [P, 2, NC, NE])
        base = sb("base", [P, 2, NC, D])
        hT = sb("hT", [P, 2, NF, SLEN])
        acc = sb("acc", [P, 2, 2, NC, D])
        res = sb("res", [P, 2, NC, D])

        ps = [ctx.enter_context(nc.psum_tensor(f"bank{i}", [P, 512], F32)) for i in range(8)]
        st_ps, v_ps = ps[1], ps[2]
        qk_banks = [ps[4] if i == 1 else ps[0] for i in range(NSEQ)]
        g_banks = [ps[5] if i == 1 else ps[3] for i in range(NSEQ)]
        fc1_ps = [ps[4], ps[5]]
        fc2_ps = ps[6]
        b_banks = [ps[2] if i == NSEQ - 1 else ps[7] for i in range(NSEQ)]

        x_dram = ins["x"].rearrange("s (c p) d -> p s c d", p=P)
        out_dram = out.rearrange("s (c p) d -> p s c d", p=P)
        block = ctx.enter_context(nc.Block())

        def score_banks(i):
            return qk_banks[i], st_ps, v_ps, g_banks[i]

        def key_product(eng, c, n):
            return eng.tensor_tensor(prod[:, c * n * D:(c + 1) * n * D].rearrange("p (t f) -> p t f", t=n),
                                     q_sb[:, c].unsqueeze(1).to_broadcast([P, n, D]), k4[:, c, 0:n, :], ALU.mult)

        def head_queries(eng, i, c, g):
            hs = slice(4 * g, 4 * g + 4)
            return eng.tensor_tensor(
                qx[:, c, hs, :], qk[:, i % 2, 0, c * P:(c + 1) * P].unsqueeze(1).to_broadcast([P, 4, P]),
                head_sel[:, hs].unsqueeze(2).to_broadcast([P, 4, P]), ALU.mult)

        def value_product(eng, c, n):
            return eng.tensor_tensor(
                prodv[:, c * n * D:(c + 1) * n * D].rearrange("p (a d) -> p a d", d=HD),
                attn_exp[:, c * n * NH:(c + 1) * n * NH].unsqueeze(2).to_broadcast([P, n * NH, HD]),
                v4[:, c, 0:n, :].rearrange("p t (h d) -> p (t h) d", d=HD), ALU.mult)

        @block.sync
        def _(eng):
            def load(name, dst, src):
                eng.dma_start(dst, src).then_inc(sem(name), 16)

            load("x0_in", x[:, 0], x_dram[:, 0])
            load("ident_in", con[:, 0:P], ins["consts"][:, 0:P])
            load("wqk_in", wqk[:], ins["wqk"].rearrange("f p n -> p f n"))
            load("con_in", con[:, P:], ins["consts"][:, P:])
            load("wvg_in", wv[:], ins["wv"])
            load("wvg_in", wg[:], ins["wg"])
            load("wo_in", wo[:], ins["wo"].rearrange("(t p) n -> p t n", p=P))
            for i in range(1, NSEQ):
                load(f"x{i}_in", x[:, i], x_dram[:, i])
                if i == 1:
                    load("wb_in", wqkv[:], ins["wqkv"])
                    load("wb_in", wproj[:], ins["wproj"])
                    load("wb_in", wrouter[:], ins["wrouter"])
                    load("wb_in", lnp[:], ins["lnp"])
                    load("rcon_in", rcon[:], ins["rconsts"])
                    load("w1_in", w1[:], ins["w1"].rearrange("e p n -> p e n"))
                    load("w2_in", w2[:], ins["w2"].rearrange("e (t p) n -> p e t n", p=P))
            for i in range(NSEQ):
                eng.wait_ge(sem("acc"), NC * NE * (i + 1))
                eng.dma_start(out_dram[:, i], res[:, i % 2]).then_inc(sem(f"stored{i % 2}"), 16)
            eng.wait_ge(sem("stored0"), 16 * NSEQ // 2)
            eng.wait_ge(sem("stored1"), 16 * NSEQ // 2)

        @block.gpsimd
        def _(eng):
            eng.memset(cum[:, 0, :], 0.0).then_inc(sem("cum0"), 1)

            def a_qx(i):
                eng.wait_ge(sem("rotated"), i + 1)
                if i == 0:
                    eng.wait_ge(sem("con_in"), 16)
                if i >= 1:
                    eng.wait_ge(sem("scores"), 4 * i)
                for c in (1, 0):
                    if c == 0 or i >= VECTOR_FIRST:
                        for g in range(2):
                            head_queries(eng, i, c, g).then_inc(sem("qx"), 1)

            def normed(o, tmp, src, mean, scale, name):
                eng.tensor_tensor(tmp, src, mean.to_broadcast([P, NC, D]), ALU.subtract).then_inc(sem(name + "_sub"), 1)
                eng.wait_ge(sem(name + "_sub"), normed_count[name] + 1)
                eng.tensor_tensor(o, tmp, scale.to_broadcast([P, NC, D]), ALU.mult).then_inc(sem(name), 1)
                normed_count[name] += 1

            normed_count = {"a_xh": 0, "hid": 0}

            def a_xh(i):
                if i < VECTOR_FIRST:
                    return
                eng.wait_ge(sem("a_rstd"), i + 1)
                if i >= 2:
                    eng.wait_ge(sem("a_T"), i - 1)
                normed(xh[:, i % 2], xh_sub[:], x[:, i], mv[:, i % 2, :, 0:1], rstd[:, i % 2].unsqueeze(2), "a_xh")

            def a_rotated(i):
                if i < VECTOR_FIRST:
                    return
                eng.wait_ge(sem("rot_b"), i + 1)
                eng.tensor_tensor(qk[:, i % 2].rearrange("p f n -> p (f n)"), rot_a[:], rot_b[:],
                                  ALU.add).then_inc(sem("rotated"), 1)

            def a_log_sigmoid(i):
                eng.wait_ge(sem("gT"), i + 1)
                if i >= 1:
                    eng.wait_ge(sem("z"), i)
                eng.tensor_scalar(gneg[:], gT[:], 0.0, None, ALU.min).then_inc(sem("g_neg"), 1)
                eng.wait_ge(sem("g_neg"), i + 1)
                eng.wait_ge(sem("g_ln"), i + 1)
                eng.tensor_tensor(gm[:], gneg[:], gl[:], ALU.subtract).then_inc(sem("g_log_sig"), 1)

            def b_hid(i):
                eng.wait_ge(sem("b_rstd"), i + 1)
                if i >= 1:
                    eng.wait_ge(sem("h1"), i)
                normed(hid[:], hid_sub[:], x1[:, i], bmv[:, :, 0:1], br[:, :, 0:1], "hid")

            def b_prod(i):
                n = i + 1
                eng.wait_ge(sem("kv4"), 5 * n)
                if i >= 1:
                    eng.wait_ge(sem("sc"), NC * i)
                for c in pool_tiles(i, PROD_SPLIT):
                    last = key_product(eng, c, n)
                last.then_inc(sem("prod"), 1)

            def a_qkc(i):
                eng.wait_ge(sem("kc1"), i + 1)
                if i >= 1:
                    eng.wait_ge(sem("rowsum"), i)
                eng.tensor_tensor(qkc[:], qk[:, i % 2, 0], kcum[:], ALU.mult).then_inc(sem("qkc"), 1)

            def a_den(i):
                eng.wait_ge(sem("s2"), i + 1)
                if i >= 1:
                    eng.wait_ge(sem("tt"), i)
                eng.tensor_scalar(den[:], s2[:], 1.0, EPS, ALU.max, ALU.mult).then_inc(sem("den"), 1)

            def b_prodv(i):
                n = i + 1
                eng.wait_ge(sem("b_exp"), n)
                if i >= 1:
                    eng.wait_ge(sem("ao"), NC * i)
                for c in pool_tiles(i, PRODV_SPLIT):
                    last = value_product(eng, c, n)
                last.then_inc(sem("prodv"), 1)

            def b_base(i):
                eng.wait_ge(sem("h1"), i + 1)
                if i >= 2:
                    eng.wait_ge(sem("acc"), NC * (NE * (i - 2) + 1))
                eng.tensor_tensor(base[:, i % 2], h1[:], x1[:, i], ALU.add).then_inc(sem("base"), 1)

            follow({"a_xh": a_xh, "a_rotated": a_rotated, "a_log_sigmoid": a_log_sigmoid, "b_hid": b_hid,
                    "b_prod": b_prod, "a_qx": a_qx, "a_qkc": a_qkc, "a_den": a_den, "b_prodv": b_prodv, "b_base": b_base})

        @block.scalar
        def _(eng):
            table = [None]

            def use(name):
                if table[0] != name:
                    eng.preload_act_table_set(name)
                    table[0] = name

            def exp_ln():
                use("natural_log_exp_and_others")

            def copy(o, i_, name):
                eng.copy(o, i_).then_inc(sem(name), 1)

            def norm_scale(o, tmp, var, ready, n, name):
                exp_ln()
                eng.wait_ge(sem(ready), n)
                eng.activation(tmp, var, ACT.Ln).then_inc(sem(name + "_ln"), 1)
                eng.wait_ge(sem(name + "_ln"), n)
                eng.activation(o, tmp, ACT.Exp, scale=-0.5).then_inc(sem(name), 1)

            def a_norm(i):
                norm_scale(rstd[:, i % 2], lnv[:, i % 2], mv[:, i % 2, :, 1], "a_var", i + 1, "a_rstd")

            def a_xT(i):
                eng.wait_ge(sem("a_T"), i + 1)
                copy(xT[:, i % 2], g_banks[i][:, 0:SLEN], "xT")

            def a_gT(i):
                eng.wait_ge(sem("vg"), i + 1)
                if i >= 1:
                    eng.wait_ge(sem("og_raw"), i)
                copy(gT[:], g_banks[i][:], "gT")
                if i >= 1:
                    eng.wait_ge(sem("g_exp"), i)
                eng.activation(ag[:], g_banks[i][:], ACT.Abs).then_inc(sem("g_abs"), 1)

            def a_sigmoid(i):
                eng.wait_ge(sem("g_abs"), i + 1)
                exp_ln()
                eng.activation(ge[:], ag[:], ACT.Exp, scale=-1.0).then_inc(sem("g_exp"), 1)
                eng.wait_ge(sem("g_exp"), i + 1)
                if i >= 1:
                    eng.wait_ge(sem("g_log_sig"), i)
                eng.activation(gl[:], ge[:], ACT.Ln, bias=1.0).then_inc(sem("g_ln"), 1)

            def a_v(i):
                eng.wait_ge(sem("vg"), i + 1)
                if i >= 2:
                    eng.wait_ge(sem("x1"), i - 1)
                copy(v[:, i % 2], v_ps[:].rearrange("p (c n) -> p c n", c=NC), "v")

            def a_knat(i):
                eng.wait_ge(sem("kT"), i + 1)
                copy(knat[:], st_ps[:, 0:P], "knat")

            def a_s2(i):
                eng.wait_ge(sem("rowsum"), i + 1)
                if i >= 1:
                    eng.wait_ge(sem("den"), i)
                eng.activation(s2[:], qk_banks[i][:], ACT.Square).then_inc(sem("s2"), 1)

            def a_osq(i):
                eng.wait_ge(sem("o"), i + 1)
                eng.activation(osq[:], qk_banks[i][:], ACT.Square).then_inc(sem("osq"), 1)

            def a_ln(i):
                exp_ln()
                eng.wait_ge(sem("tt"), i + 1)
                eng.activation(lt[:], tt[:], ACT.Ln).then_inc(sem("lt"), 1)

            def a_weight(i):
                exp_ln()
                eng.wait_ge(sem("z"), i + 1)
                eng.activation(wgt[:], z[:], ACT.Exp).then_inc(sem("wgt"), 1)

            def b_norm(i):
                norm_scale(br[:], bln[:], bv2[:], "b_var", i + 1, "b_rstd")

            def b_l1T(i):
                eng.wait_ge(sem("b_T"), i + 1)
                eng.wait_ge(sem("wb_in"), 64)
                eng.activation(l1T[:], b_banks[i][:, 0:SLEN], ACT.Identity, bias=lnp[:, 1:2],
                               scale=lnp[:, 0:1]).then_inc(sem("l1T"), 1)

            def b_kv(i):
                eng.wait_ge(sem("qkv"), i + 1)
                if i >= 1:
                    eng.wait_ge(sem("prod"), i)
                    if i > PROD_SPLIT:
                        eng.wait_ge(sem("prod_v"), i - PROD_SPLIT)
                copy(q_sb[:], b_banks[i][:, 0:2 * 192].rearrange("p (c n) -> p c n", c=NC)[:, :, 0:D], "kv4")
                for c in range(NC):
                    for dst, off in ((k4, D), (v4, D + KVD)):
                        src = b_banks[i][:, c * 192 + off:c * 192 + off + KVD]
                        src = src.rearrange("p (g d) -> p g d", d=HD).unsqueeze(2)
                        copy(dst[:, c, i].rearrange("p (g r d) -> p g r d", g=NKV, r=QPK),
                             src.to_broadcast([P, NKV, QPK, HD]), "kv4")

            def b_exp(i):
                exp_ln()
                n = NC * (i + 1) * NH
                eng.wait_ge(sem("scm"), i + 1)
                if i >= 1:
                    eng.wait_ge(sem("prodv"), i)
                    eng.wait_ge(sem("ssum"), i)
                    if i > PRODV_SPLIT:
                        eng.wait_ge(sem("prodv_v"), i - PRODV_SPLIT)
                eng.activation(attn_exp[:, 0:n], scm[:, 0:n], ACT.Exp, scale=HD ** -0.5).then_inc(sem("b_exp"), 1)

            def b_aoT(i):
                eng.wait_ge(sem("aoT_ps"), i + 1)
                copy(aoT[:], b_banks[i][:, 0:SLEN], "aoT")

            def c_norm(i):
                norm_scale(cr[:], cln[:], cv[:], "c_var", i + 1, "c_rstd")

            def c_x2T(i):
                eng.wait_ge(sem("c_T"), i + 1)
                eng.wait_ge(sem("wb_in"), 64)
                if i >= 2:
                    eng.wait_ge(sem("fc1"), NE * (i - 1))
                eng.activation(x2T[:, i % 2], b_banks[i][:, 0:SLEN], ACT.Identity, bias=lnp[:, 3:4],
                               scale=lnp[:, 2:3]).then_inc(sem("x2T"), 1)

            def c_exp(i):
                exp_ln()
                eng.wait_ge(sem("lsub"), i + 1)
                eng.activation(pr[:], lsub[:], ACT.Exp).then_inc(sem("pr"), 1)

            def m_gelu(i, e):
                n = NE * i + e
                use("gelu_apprx_tanh_and_others")
                eng.wait_ge(sem("fc1"), n + 1)
                if n >= 2:
                    eng.wait_ge(sem("fc2"), n - 1)
                eng.activation(hT[:, n % 2], fc1_ps[n % 2][:].rearrange("p (t n) -> p t n", t=NF),
                               ACT.Gelu_apprx_tanh).then_inc(sem("gelu"), 1)

            stages = {
                "a_rstd": a_norm, "a_xT": a_xT, "a_v": a_v, "a_gT": a_gT, "a_sigmoid": a_sigmoid,
                "a_knat": a_knat, "a_s2": a_s2, "a_osq": a_osq, "a_ln": a_ln, "a_weight": a_weight,
                "b_rstd": b_norm, "b_l1T": b_l1T, "b_kv4": b_kv, "b_exp": b_exp, "b_aoT": b_aoT,
                "c_rstd": c_norm, "c_x2T": c_x2T, "c_exp": c_exp,
            }
            for e in range(NE):
                stages[f"m_gelu_{e}"] = lambda i, e=e: m_gelu(i, e)
            follow(stages)

        @block.tensor
        def _(eng):
            mm = eng.matmul

            def a_T(i):
                if i < VECTOR_FIRST:
                    eng.wait_ge(sem("a_xh_v"), NC * (i + 1))
                else:
                    eng.wait_ge(sem("a_xh"), i + 1 - VECTOR_FIRST)
                if i == 0:
                    eng.wait_ge(sem("ident_in"), 16)
                if i >= 2:
                    eng.wait_ge(sem("sm"), 4 * i)
                for c in range(NC):
                    last = eng.transpose(g_banks[i][:, c * P:(c + 1) * P], xh[:, i % 2, c], ident)
                last.then_inc(sem("a_T"), 1)

            def a_qk(i):
                eng.wait_ge(sem("xT"), i + 1)
                t = xT[:, i % 2]
                if i == 0:
                    eng.wait_ge(sem("wqk_in"), 16)
                if i >= 2:
                    eng.wait_ge(sem("og_raw"), i)
                    eng.wait_ge(sem("tt"), i)
                for f in range(2):
                    last = mm(qk_banks[i][:, f * SLEN:(f + 1) * SLEN], wqk[:, f], t,
                              start=True, stop=True)
                last.then_inc(sem("qk"), 1)

            def a_vg(i):
                t = xT[:, i % 2]
                if i == 0:
                    eng.wait_ge(sem("wvg_in"), 32)
                if i >= 1:
                    eng.wait_ge(sem("x1"), i)
                for c in range(NC):
                    mm(v_ps[:, c * VD:(c + 1) * VD], t[:, c * P:(c + 1) * P], wv[:], start=True, stop=True)
                for u in range(2):
                    last = mm(g_banks[i][:, u * SLEN:(u + 1) * SLEN], wg[:, u * P:(u + 1) * P], t,
                              start=True, stop=True)
                last.then_inc(sem("vg"), 1)

            def a_kT(i):
                eng.wait_ge(sem("rotated"), i + 1)
                if i >= 1:
                    eng.wait_ge(sem("tt"), i)
                eng.transpose(st_ps[:, 0:P], qk[:, i % 2, 1, 0:P], ident).then_inc(sem("kT"), 1)

            def a_rowsums(i):
                eng.wait_ge(sem("qkc"), i + 1)
                if i == 0:
                    eng.wait_ge(sem("con_in"), 16)
                if i == 1:
                    eng.wait_ge(sem("og_raw"), i)
                    eng.wait_ge(sem("tt"), i)
                for u in range(2):
                    last = mm(qk_banks[i][:, u * SLEN:(u + 1) * SLEN], same_head[:, u * P:(u + 1) * P], qkc[:],
                              start=True, stop=True)
                last.then_inc(sem("rowsum"), 1)

            def a_state_mm(i):
                eng.wait_ge(sem("knat"), i + 1)
                eng.wait_ge(sem("v"), i + 1)
                mm(st_ps[:, P:P + VD], knat[:], v[:, i % 2, 0], start=True, stop=True).then_inc(sem("state_ps"), 1)

            def a_scores(i):
                for n, (c, g) in enumerate([(1, 0), (1, 1), (0, 0), (0, 1)]):
                    if n == 0:
                        eng.wait_ge(sem("v"), i + 1)
                        eng.wait_ge(sem("g_abs"), i + 1)
                    if n == 2:
                        eng.wait_ge(sem("s2"), i + 1)
                        eng.wait_ge(sem("state"), i + 1)
                    if c == 1 and i < VECTOR_FIRST:
                        eng.wait_ge(sem("qx_v"), 2 * i + g + 1)
                    elif i < VECTOR_FIRST:
                        eng.wait_ge(sem("qx"), 2 * i + g + 1)
                    else:
                        eng.wait_ge(sem("qx"), 4 * i - 2 * VECTOR_FIRST + n + 1)
                    mm(score_banks(i)[2 * c + g][:], qk[:, i % 2, 1, c * P:(c + 1) * P],
                       qx[:, c, 4 * g:4 * g + 4, :], start=True, stop=True).then_inc(sem("scores"), 1)

            def a_out(i):
                eng.wait_ge(sem("sm"), 4 * (i + 1))
                for u in range(2):
                    mm(qk_banks[i][:, u * SLEN + P:(u + 1) * SLEN], state[:, u * P:(u + 1) * P],
                       qk[:, i % 2, 0, P:SLEN], start=(u == 0), stop=False, skip_group_check=True)
                for c in range(NC):
                    for h in range(RH):
                        u, r = h // 4, h % 4
                        last = mm(qk_banks[i][32 * r:32 * r + 32, u * SLEN + c * P:u * SLEN + (c + 1) * P],
                                  v[:, i % 2, c, h * RV:(h + 1) * RV], sm[:, c, h, :],
                                  start=False, stop=(c == NC - 1 and u == 1), skip_group_check=True)
                last.then_inc(sem("o"), 1)

            def a_ms(i):
                eng.wait_ge(sem("osq"), i + 1)
                mm(st_ps[:], head_mean, osq[:], start=True, stop=True).then_inc(sem("ms"), 1)

            def a_wo(i):
                eng.wait_ge(sem("og"), i + 1)
                if i == 0:
                    eng.wait_ge(sem("wo_in"), 16)
                for c in range(NC):
                    for u in range(2):
                        last = mm(v_ps[:, c * D:(c + 1) * D], og[:, u * SLEN + c * P:u * SLEN + (c + 1) * P],
                                  wo[:, u], start=(u == 0), stop=(u == 1))
                last.then_inc(sem("wo"), 1)

            def b_T(i):
                eng.wait_ge(sem("b_core"), NC * (i + 1))
                if 1 <= i < NSEQ - 1:
                    eng.wait_ge(sem("gate"), i)
                for c in range(NC):
                    last = eng.transpose(b_banks[i][:, c * P:(c + 1) * P], core[:, c], ident)
                last.then_inc(sem("b_T"), 1)

            def b_qkv(i):
                eng.wait_ge(sem("l1T"), i + 1)
                for c in range(NC):
                    last = mm(b_banks[i][:, c * 192:(c + 1) * 192], l1T[:, c * P:(c + 1) * P], wqkv[:],
                              start=True, stop=True)
                last.then_inc(sem("qkv"), 1)

            def b_aoT(i):
                eng.wait_ge(sem("aon"), i + 1)
                for c in range(NC):
                    last = eng.transpose(b_banks[i][:, c * P:(c + 1) * P], aon[:, c], ident)
                last.then_inc(sem("aoT_ps"), 1)

            def b_proj(i):
                eng.wait_ge(sem("aoT"), i + 1)
                for c in range(NC):
                    last = mm(b_banks[i][:, SLEN + c * P:SLEN + (c + 1) * P], aoT[:, c * P:(c + 1) * P], wproj[:],
                              start=True, stop=True)
                last.then_inc(sem("proj"), 1)

            def c_T(i):
                eng.wait_ge(sem("core2"), NC * (i + 1))
                for c in range(NC):
                    last = eng.transpose(b_banks[i][:, c * P:(c + 1) * P], core2[:, c], ident)
                last.then_inc(sem("c_T"), 1)

            def c_router(i):
                eng.wait_ge(sem("x2T"), i + 1)
                for c in range(NC):
                    last = mm(b_banks[i][:, SLEN + c * NE:SLEN + (c + 1) * NE], x2T[:, i % 2, c * P:(c + 1) * P],
                              wrouter[:], start=True, stop=True)
                last.then_inc(sem("logits"), 1)

            def c_rank(i):
                eng.wait_ge(sem("cum"), NC * (i + 1))
                for c in range(NC):
                    o = b_banks[i][:, SLEN + (NC + c) * NE:SLEN + (NC + c + 1) * NE]
                    mm(o, before[:, 0:P], selb[:, c], start=True, stop=False)
                    last = mm(o, before[:, P:], cum[:, NC * i + c, :], start=False, stop=True)
                last.then_inc(sem("rank"), 1)

            def m_fc1(i, e):
                n = NE * i + e
                if n >= 2:
                    eng.wait_ge(sem("gelu"), n - 1)
                if n == 0:
                    eng.wait_ge(sem("w1_in"), 16)
                    eng.wait_ge(sem("og_raw"), 2)
                if n == 1:
                    eng.wait_ge(sem("sm"), 4 * 2)
                if e == 0:
                    eng.wait_ge(sem("x2T"), i + 1)
                for t in range(NF):
                    last = mm(fc1_ps[n % 2][:, t * SLEN:(t + 1) * SLEN], w1[:, e, t * P:(t + 1) * P],
                              x2T[:, i % 2], start=True, stop=True)
                last.then_inc(sem("fc1"), 1)

            def m_fc2(i, e):
                n = NE * i + e
                eng.wait_ge(sem("gelu"), n + 1)
                if n == 0:
                    eng.wait_ge(sem("w2_in"), 16)
                if n >= 1:
                    eng.wait_ge(sem("acc"), NC * n)
                for c in range(NC):
                    for t in range(NF):
                        last = mm(fc2_ps[:, (n % 2) * SLEN + c * D:(n % 2) * SLEN + (c + 1) * D],
                                  hT[:, n % 2, t, c * P:(c + 1) * P], w2[:, e, t],
                                  start=(t == 0), stop=(t == NF - 1))
                last.then_inc(sem("fc2"), 1)

            stages = {
                "a_T": a_T, "a_qk": a_qk, "a_vg": a_vg, "a_kT": a_kT, "a_rowsums": a_rowsums,
                "a_state_mm": a_state_mm, "a_scores": a_scores, "a_out": a_out, "a_ms": a_ms, "a_wo": a_wo,
                "b_T": b_T, "b_qkv": b_qkv, "b_aoT_mm": b_aoT, "b_proj": b_proj,
                "c_T": c_T, "c_logits": c_router, "c_rank": c_rank,
            }
            for e in range(NE):
                stages[f"m_fc1_{e}"] = lambda i, e=e: m_fc1(i, e)
                stages[f"m_fc2_{e}"] = lambda i, e=e: m_fc2(i, e)
            follow(stages)

        @block.vector
        def _(eng):
            count = {}

            def done(ins_, name):
                ins_.then_inc(sem(name), 1)
                count[name] = count.get(name, 0) + 1

            def after(*names):
                for name in names:
                    eng.wait_ge(sem(name), count[name])

            tt_, ts_ = eng.tensor_tensor, eng.tensor_scalar

            def statistics(src, st, name):
                for c in range(NC):
                    done(eng.bn_stats(st[:, c], src[:, c]), name)

            def moments(st, out_, stat_name, name):
                after(stat_name)
                for c in range(NC):
                    done(eng.bn_aggr(out_[:, c], st[:, c]), name)

            def a_stats(i):
                eng.wait_ge(sem(f"x{i}_in"), 16)
                statistics(x[:, i], stat[:, i % 2], "a_stat")

            def a_moments(i):
                moments(stat[:, i % 2], mv[:, i % 2], "a_stat", "a_aggr")

            def a_var(i):
                after("a_aggr")
                done(ts_(mv[:, i % 2, :, 1], mv[:, i % 2, :, 1], EPS, None, ALU.add), "a_var")

            def a_rotate(i):
                eng.wait_ge(sem("qk"), i + 1)
                if i >= 1:
                    eng.wait_ge(sem("rotated"), i)
                if i == 0:
                    eng.wait_ge(sem("con_in"), 16)
                done(eng.stream_shuffle(swapped[:], qk_banks[i][:], [p ^ 1 for p in range(32)]), "swapped")
                done(tt_(rot_a[:], qk_banks[i][:], cos_t, ALU.mult), "rot_a")
                after("swapped")
                done(tt_(rot_b[:], swapped[:], sin_t, ALU.mult), "rot_b")
                if i < VECTOR_FIRST:
                    after("rot_a", "rot_b")
                    done(tt_(qk[:, i % 2].rearrange("p f n -> p (f n)"), rot_a[:], rot_b[:], ALU.add), "rotated")

            def a_xh(i):
                if i < VECTOR_FIRST:
                    eng.wait_ge(sem("a_rstd"), i + 1)
                    for c in range(NC):
                        done(ts_(xh[:, i % 2, c], x[:, i, c], mv[:, i % 2, c, 0:1], rstd[:, i % 2, c:c + 1],
                                 ALU.subtract, ALU.mult), "a_xh_v")

            def a_qx(i):
                if i < VECTOR_FIRST:
                    if i >= 1:
                        eng.wait_ge(sem("scores"), 4 * i)
                    for g in range(2):
                        done(head_queries(eng, i, 1, g), "qx_v")

            def a_kcum(i):
                eng.wait_ge(sem("rotated"), i + 1)
                if i >= 1:
                    eng.wait_ge(sem("qkc"), i)
                k = qk[:, i % 2, 1]
                done(eng.tensor_tensor_scan(kcum[:, 0:P], ones, k[:, 0:P], 0.0, ALU.mult, ALU.add), "kc0")
                after("kc0")
                done(tt_(kinit[:], kcum[:, P - 1:P], chunk_decay, ALU.mult), "kinit")
                after("kinit")
                done(eng.tensor_tensor_scan(kcum[:, P:SLEN], ones, k[:, P:SLEN], kinit[:], ALU.mult, ALU.add), "kc1")

            def a_state(i):
                eng.wait_ge(sem("state_ps"), i + 1)
                done(tt_(state[:], st_ps[:, P:P + VD], state_mask, ALU.mult), "state")

            def a_mask(i):
                for n, (c, g) in enumerate([(1, 0), (1, 1), (0, 0), (0, 1)]):
                    eng.wait_ge(sem("scores"), 4 * i + n + 1)
                    done(tt_(sm[:, c, 4 * g:4 * g + 4, :], score_banks(i)[2 * c + g][:].rearrange("p (h n) -> p h n", h=4),
                             tri.unsqueeze(1).to_broadcast([P, 4, P]), ALU.mult), "sm")

            def a_scale_in(i):
                eng.wait_ge(sem("ms"), i + 1)
                eng.wait_ge(sem("den"), i + 1)
                done(tt_(tt[:], st_ps[:], den[:], ALU.add), "tt")

            def a_z(i):
                eng.wait_ge(sem("lt"), i + 1)
                eng.wait_ge(sem("g_log_sig"), i + 1)
                done(eng.scalar_tensor_tensor(z[:], lt[:], -0.5, gm[:], ALU.mult, ALU.add), "z")

            def a_og_raw(i):
                eng.wait_ge(sem("osq"), i + 1)
                eng.wait_ge(sem("gT"), i + 1)
                done(tt_(og[:], qk_banks[i][:], gT[:], ALU.mult), "og_raw")

            def a_og(i):
                eng.wait_ge(sem("wgt"), i + 1)
                after("og_raw")
                done(tt_(og[:], og[:], wgt[:], ALU.mult), "og")

            def a_x1(i):
                eng.wait_ge(sem("wo"), i + 1)
                done(tt_(x1[:, i], v_ps[:, 0:SLEN].rearrange("p (c n) -> p c n", c=NC), x[:, i], ALU.add), "x1")

            def b_stats(i):
                after("x1")
                statistics(x1[:, i], bstat, "b_stat")

            def b_moments(i):
                if i >= 1:
                    eng.wait_ge(sem("hid"), i)
                moments(bstat, bmv, "b_stat", "b_aggr")

            def b_var(i):
                after("b_aggr")
                done(ts_(bv2[:, :, 0], bmv[:, :, 1], EPS, None, ALU.add), "b_var0")
                done(ts_(bv2[:, :, 1], bmv[:, :, 1], 1.0 + EPS, EPS * EPS, ALU.mult, ALU.add), "b_var")

            def b_core(i):
                eng.wait_ge(sem("b_rstd"), i + 1)
                for c in range(NC):
                    done(ts_(core[:, c], x1[:, i, c], bmv[:, c, 0:1], br[:, c, 1:2],
                             ALU.subtract, ALU.mult), "b_core")

            def b_scores(i):
                n = i + 1
                if i >= PROD_SPLIT:
                    eng.wait_ge(sem("kv4"), 5 * n)
                    done(key_product(eng, 0, n), "prod_v")
                    after("prod_v")
                for c in range(NC):
                    if c in pool_tiles(i, PROD_SPLIT):
                        eng.wait_ge(sem("prod"), n)
                    pv = prod[:, c * n * D:(c + 1) * n * D].rearrange("p (a d) -> p a d", d=HD)
                    done(eng.tensor_reduce(sc[:, c * n * NH:(c + 1) * n * NH], pv, X, ALU.add), "sc")

            def b_scores2(i):
                n = i + 1
                after("sc")
                s = sc[:, 0:NC * n * NH].rearrange("p (c t h) -> p c t h", c=NC, t=n)
                done(eng.tensor_reduce(mx[:], s.rearrange("p c t h -> p c h t"), X, ALU.max), "mx")
                after("mx")
                done(tt_(scm[:, 0:NC * n * NH].rearrange("p (c t h) -> p c t h", c=NC, t=n), s,
                         mx[:].unsqueeze(2).to_broadcast([P, NC, n, NH]), ALU.subtract), "scm")

            def b_sum(i):
                n = i + 1
                eng.wait_ge(sem("b_exp"), n)
                e = attn_exp[:, 0:NC * n * NH]
                if i >= PRODV_SPLIT:
                    after("ao")
                    done(value_product(eng, 0, n), "prodv_v")
                done(eng.tensor_reduce(ssum[:], e.rearrange("p (c t h) -> p c h t", c=NC, t=n), X, ALU.add), "ssum")
                after("ssum")
                done(eng.reciprocal(rsum[:], ssum[:]), "rsum")

            def b_ao(i):
                n = i + 1
                if i >= PRODV_SPLIT:
                    after("prodv_v")
                for c in range(NC):
                    if c in pool_tiles(i, PRODV_SPLIT):
                        eng.wait_ge(sem("prodv"), n)
                    pv = prodv[:, c * n * D:(c + 1) * n * D].rearrange("p (t f) -> p f t", t=n)
                    done(eng.tensor_reduce(ao[:, c], pv, X, ALU.add), "ao")

            def b_norm(i):
                after("ao", "rsum")
                done(tt_(aon[:].rearrange("p c (h d) -> p (c h) d", d=HD),
                         ao[:].rearrange("p c (h d) -> p (c h) d", d=HD),
                         rsum[:].rearrange("p c h -> p (c h)").unsqueeze(2).to_broadcast([P, NC * NH, HD]),
                         ALU.mult), "aon")

            def c_h1(i):
                eng.wait_ge(sem("proj"), i + 1)
                eng.wait_ge(sem("hid"), i + 1)
                done(tt_(h1[:], b_banks[i][:, SLEN:2 * SLEN].rearrange("p (c n) -> p c n", c=NC), hid[:], ALU.add), "h1")

            def c_stats(i):
                after("h1")
                statistics(h1, cstat, "c_stat")

            def c_moments(i):
                moments(cstat, cmv, "c_stat", "c_aggr")

            def c_var(i):
                after("c_aggr")
                done(ts_(cv[:], cmv[:, :, 1], EPS, None, ALU.add), "c_var")

            def c_core(i):
                eng.wait_ge(sem("c_rstd"), i + 1)
                for c in range(NC):
                    done(ts_(core2[:, c], h1[:, c], cmv[:, c, 0:1], cr[:, c:c + 1],
                             ALU.subtract, ALU.mult), "core2")

            def c_lsub(i):
                eng.wait_ge(sem("logits"), i + 1)
                lg = b_banks[i][:, SLEN:SLEN + NC * NE].rearrange("p (c e) -> p c e", c=NC)
                done(eng.tensor_reduce(lmx[:], lg, X, ALU.max), "lmx")
                after("lmx")
                done(tt_(lsub[:], lg, lmx[:].unsqueeze(2).to_broadcast([P, NC, NE]), ALU.subtract), "lsub")

            def c_place(i):
                if i == 0:
                    eng.wait_ge(sem("rcon_in"), 16)
                    done(eng.tensor_copy(before[:], rcon[:, 0:2 * P]), "before")
                    eng.wait_ge(sem("cum0"), 1)
                eng.wait_ge(sem("pr"), i + 1)
                for c in range(NC):
                    mine = pr[:, c].unsqueeze(2).to_broadcast([P, NE, NE])
                    other = pr[:, c].unsqueeze(1).to_broadcast([P, NE, NE])
                    done(tt_(cgt[:, c], other, mine, ALU.is_gt), "cgt")
                    done(tt_(cge[:, c], other, mine, ALU.is_ge), "cge")

            def c_ties(i):
                low = lower.rearrange("p (e j) -> p e j", e=NE)
                after("cge")
                done(tt_(cgl[:], cge[:], low.unsqueeze(1).to_broadcast([P, NC, NE, NE]), ALU.mult), "cgl")

            def c_or(i):
                after("cgl")
                done(tt_(cor[:], cgl[:], cgt[:], ALU.max), "cor")

            def c_count(i):
                after("cor")
                done(eng.tensor_reduce(place[:], cor[:], X, ALU.add), "place")

            def c_select(i):
                after("place")
                done(ts_(selb[:], place[:], TOPK - 0.5, None, ALU.is_lt), "selb")
                done(ts_(sel[:], place[:], TOPK - 0.5, None, ALU.is_lt), "sel")
                after("sel")
                for c in range(NC):
                    n = NC * i + c
                    done(tt_(cum[:, n + 1, :], cum[:, n, :], selb[:, c], ALU.add), "cum")
                    after("cum")

            def c_chosen(i):
                after("sel")
                done(tt_(chosen[:], pr[:], sel[:], ALU.mult), "chosen")

            def c_sum(i):
                after("chosen")
                done(eng.tensor_reduce(csum[:], chosen[:], X, ALU.add), "csum")

            def c_rec(i):
                after("csum")
                done(eng.reciprocal(crec[:], csum[:]), "crec")

            def c_gsel(i):
                after("crec")
                done(tt_(gsel[:], chosen[:], crec[:].unsqueeze(2).to_broadcast([P, NC, NE]), ALU.mult), "gsel")

            def c_gate(i):
                eng.wait_ge(sem("rank"), i + 1)
                rk = b_banks[i][:, SLEN + NC * NE:SLEN + 2 * NC * NE].rearrange("p (c e) -> p c e", c=NC)
                done(ts_(fits[:], rk, CAP - 0.5, None, ALU.is_lt), "fits")
                after("fits", "gsel")
                done(tt_(gate[:, i % 2], gsel[:], fits[:], ALU.mult), "gate")

            def m_acc(i, e):
                n = NE * i + e
                eng.wait_ge(sem("fc2"), n + 1)
                if e == 0:
                    after("gate")
                    eng.wait_ge(sem("base"), i + 1)
                else:
                    after("acc")
                if e == NE - 1 and i >= 2:
                    eng.wait_ge(sem(f"stored{i % 2}"), 16 * (i // 2))
                for c in range(NC):
                    o = fc2_ps[:, (n % 2) * SLEN + c * D:(n % 2) * SLEN + (c + 1) * D]
                    prev = base[:, i % 2, c] if e == 0 else acc[:, i % 2, (e - 1) % 2, c]
                    dst = res[:, i % 2, c] if e == NE - 1 else acc[:, i % 2, e % 2, c]
                    done(eng.scalar_tensor_tensor(dst, o, gate[:, i % 2, c, e:e + 1], prev,
                                                  ALU.mult, ALU.add), "acc")

            stages = {
                "a_xh": a_xh, "a_qx": a_qx, "a_stats": a_stats, "a_moments": a_moments, "a_var": a_var, "a_rotate": a_rotate, "a_kcum": a_kcum,
                "a_state": a_state, "a_mask": a_mask, "a_scale_in": a_scale_in, "a_z": a_z,
                "a_og_raw": a_og_raw, "a_og": a_og, "a_x1": a_x1,
                "b_stats": b_stats, "b_moments": b_moments, "b_var": b_var, "b_core": b_core,
                "b_scores": b_scores, "b_scores2": b_scores2, "b_sum": b_sum, "b_ao": b_ao,
                "b_norm": b_norm, "b_h1": c_h1,
                "c_stats": c_stats, "c_moments": c_moments, "c_var": c_var, "c_core": c_core,
                "c_lsub": c_lsub, "c_place": c_place, "c_ties": c_ties, "c_or": c_or, "c_count": c_count,
                "c_select": c_select, "c_chosen": c_chosen, "c_sum": c_sum, "c_rec": c_rec,
                "c_gsel": c_gsel, "c_gate": c_gate,
            }
            for e in range(NE):
                stages[f"m_acc_{e}"] = lambda i, e=e: m_acc(i, e)
            follow(stages)


def lay_out(a):
    f = lambda n: np.ascontiguousarray(np.asarray(a[n]))
    per = f("L0_ffn_qkv_weight").reshape(NKV, (QPK + 2) * HD, D)
    q, k, v = per[:, :QPK * HD], per[:, QPK * HD:(QPK + 1) * HD], per[:, (QPK + 1) * HD:]
    return {
        "x": f("L0_attn_x"),
        "consts": retention_constants(),
        "rconsts": routing_constants(),
        "wqk": np.stack([f("L0_attn_wq"), f("L0_attn_wk")]),
        "wv": f("L0_attn_wv"), "wg": f("L0_attn_wg"), "wo": f("L0_attn_wo"),
        "wqkv": np.concatenate([t.reshape(-1, D) for t in (q, k, v)]).T,
        "wproj": f("L0_ffn_proj_weight").T,
        "wrouter": f("L0_ffn_router_weight"),
        "lnp": np.stack([f("L0_ffn_ln1_weight"), f("L0_ffn_ln1_bias"), f("L0_ffn_ln2_weight"), f("L0_ffn_ln2_bias")], 1),
        "w1": f("L0_ffn_moe_w1"), "w2": f("L0_ffn_moe_w2"),
    }


def kernel(**inputs):
    import concourse.bacc as _bacc
    from concourse.bass_utils import run_bass_kernel_spmd as _run

    nc = _bacc.Bacc("TRN2", target_bir_lowering=False, num_devices=1)
    arrays = {f"in_{n}": np.ascontiguousarray(a) for n, a in lay_out(inputs).items()}
    ins = {n[3:]: nc.dram_tensor(n, a.shape, mybir.dt.from_np(a.dtype), kind="ExternalInput").ap()
           for n, a in arrays.items()}
    out = nc.dram_tensor("out", (NSEQ, SLEN, D), F32, kind="ExternalOutput").ap()
    build(nc, ins, out)
    r = _run(nc, [arrays], core_ids=[0])
    return r.results[0]["out"]
```
